# Optimizing a Trainium2 kernel written in Bass

```python
import numpy as np
import jax
import jax.numpy as jnp

def _softmax(x, axis=-1):
    return jax.nn.softmax(x, axis=axis)

def _gelu(x):
    return jax.nn.gelu(x, approximate=True)

def _silu(x):
    return jax.nn.silu(x)

def _sigmoid(x):
    return jax.nn.sigmoid(x)

def _layernorm(x, axis=-1, eps=1e-05):
    m = jnp.mean(x, axis=axis, keepdims=True)
    v = jnp.var(x, axis=axis, keepdims=True)
    return (x - m) / jnp.sqrt(v + eps)

def _scatter_add(tgt, idx, src, axis=0):
    return tgt.at[idx].add(src)

def _segment_sum(src, seg, n):
    return jax.ops.segment_sum(src, seg, n)
kernel_name = 'mk_xattn_ffn_d1_seqx_r8_1266e3'

def setup_inputs(seed: int=0):
    np.random.seed(seed)
    _w = jnp.asarray

    def _rec_inputs():
        import jax
        import jax.numpy as jnp
        _rk = jax.random.key(seed)
        x = 7.22e-05 + 1 * jax.random.normal(jax.random.fold_in(_rk, 1), (16, 100, 256), jnp.float32)
        _lenS = 100 - jax.random.randint(jax.random.fold_in(_rk, 7), (16,), 0, max(1, 100 // 4) + 1, jnp.int32)
        _lenS2 = 1444 - jax.random.randint(jax.random.fold_in(_rk, 8), (16,), 0, max(1, 1444 // 4) + 1, jnp.int32)
        _ctx_2048P = jax.random.normal(jax.random.fold_in(_rk, 11), (16, 16, 256), jnp.float32)
        _ctx_2048c = jax.random.dirichlet(jax.random.fold_in(_rk, 511), 0.3 * jnp.ones((16,), jnp.float32), (16, 1444))
        _ctx_2048t = jnp.einsum('bsk,bkd->bsd', _ctx_2048c, _ctx_2048P)
        _ctx_2048t = _ctx_2048t * jax.lax.rsqrt(jnp.mean(jnp.square(_ctx_2048t)) + 1e-12) * 0.953939
        ctx_2048 = -0.000514642 + 1.00011 * (_ctx_2048t + 0.3 * jax.random.normal(jax.random.fold_in(_rk, 611), (16, 1444, 256), jnp.float32))
        return (x, ctx_2048)
    x, ctx_2048 = _rec_inputs()

    def _L0_xattn_setup():
        import jax, jax.numpy as jnp
        import numpy as np
        D_MODEL = 256
        NUM_HEADS = 16
        HEAD_DIM = D_MODEL // NUM_HEADS

        def _fq_sym(x, axis):
            s = jnp.max(jnp.abs(x), axis=axis, keepdims=True) / 127.0
            s = jnp.maximum(s, 1e-08)
            q = jnp.clip(jnp.round(x / s), -127.0, 127.0) * s
            return x + jax.lax.stop_gradient(q - x)

        def _fq_unsigned(x, axis):
            s = jnp.max(x, axis=axis, keepdims=True) / 255.0
            s = jnp.maximum(s, 1e-08)
            q = jnp.clip(jnp.round(x / s), 0.0, 255.0) * s
            return x + jax.lax.stop_gradient(q - x)
        key = jax.random.key(seed)
        ks = jax.random.split(key, 8)
        B, N, M, C = (2, 256, 64, D_MODEL)
        return {'x': jax.random.normal(ks[0], (B, N, C), jnp.float32), 'cond': jax.random.normal(ks[1], (B, M, C), jnp.float32), 'Wq': jax.random.normal(ks[2], (C, C), jnp.float32) * 0.02, 'bq': jnp.zeros((C,), jnp.float32), 'Wkv': jax.random.normal(ks[3], (C, 2 * C), jnp.float32) * 0.02, 'bkv': jnp.zeros((2 * C,), jnp.float32), 'Wp': jax.random.normal(ks[4], (C, C), jnp.float32) * 0.02, 'bp': jnp.zeros((C,), jnp.float32)}
    _L0_xattn_all = _L0_xattn_setup()
    _L0_xattn_in = {k: v for k, v in _L0_xattn_all.items() if k in ('Wq', 'bq', 'Wkv', 'bkv', 'Wp', 'bp')}
    del _L0_xattn_all

    def _L0_ffn_setup():
        import jax, jax.numpy as jnp
        import numpy as np
        H = 256
        I = 176
        E = 16
        K = 2
        SI = I * 2

        def _swiglu(gu, inter):
            g, u = (gu[..., :inter], gu[..., inter:])
            return jax.nn.silu(g) * u
        key = jax.random.key(seed)
        ks = jax.random.split(key, 6)
        s = 0.02
        hidden_states = jax.random.normal(ks[0], (1, 128, H), dtype=jnp.float32)
        gate_w = jax.random.normal(ks[1], (E, H), dtype=jnp.float32) * s
        w_gate_up = jax.random.normal(ks[2], (E, H, 2 * I), dtype=jnp.float32) * s
        w_down = jax.random.normal(ks[3], (E, I, H), dtype=jnp.float32) * s
        shared_gate_up = jax.random.normal(ks[4], (H, 2 * SI), dtype=jnp.float32) * s
        shared_down = jax.random.normal(ks[5], (SI, H), dtype=jnp.float32) * s
        return {'hidden_states': hidden_states, 'gate_w': gate_w, 'w_gate_up': w_gate_up, 'w_down': w_down, 'shared_gate_up': shared_gate_up, 'shared_down': shared_down}
    _L0_ffn_all = _L0_ffn_setup()
    _L0_ffn_in = {k: v for k, v in _L0_ffn_all.items() if k in ('gate_w', 'w_gate_up', 'w_down', 'shared_gate_up', 'shared_down')}
    del _L0_ffn_all
    return {'x': x, 'ctx_2048': ctx_2048, 'L0_xattn_Wq': _L0_xattn_in['Wq'], 'L0_xattn_bq': _L0_xattn_in['bq'], 'L0_xattn_Wkv': _L0_xattn_in['Wkv'], 'L0_xattn_bkv': _L0_xattn_in['bkv'], 'L0_xattn_Wp': _L0_xattn_in['Wp'], 'L0_xattn_bp': _L0_xattn_in['bp'], 'L0_ffn_gate_w': _L0_ffn_in['gate_w'], 'L0_ffn_w_gate_up': _L0_ffn_in['w_gate_up'], 'L0_ffn_w_down': _L0_ffn_in['w_down'], 'L0_ffn_shared_gate_up': _L0_ffn_in['shared_gate_up'], 'L0_ffn_shared_down': _L0_ffn_in['shared_down']}

def reference(x, ctx_2048, L0_xattn_Wq, L0_xattn_bq, L0_xattn_Wkv, L0_xattn_bkv, L0_xattn_Wp, L0_xattn_bp, L0_ffn_gate_w, L0_ffn_w_gate_up, L0_ffn_w_down, L0_ffn_shared_gate_up, L0_ffn_shared_down):
    import jax
    import jax.numpy as jnp

    def _L0_xattn_ref(x, cond, Wq, bq, Wkv, bkv, Wp, bp):
        import jax, jax.numpy as jnp
        import numpy as np
        D_MODEL = 256
        NUM_HEADS = 16
        HEAD_DIM = D_MODEL // NUM_HEADS

        def _fq_sym(x, axis):
            s = jnp.max(jnp.abs(x), axis=axis, keepdims=True) / 127.0
            s = jnp.maximum(s, 1e-08)
            q = jnp.clip(jnp.round(x / s), -127.0, 127.0) * s
            return x + jax.lax.stop_gradient(q - x)

        def _fq_unsigned(x, axis):
            s = jnp.max(x, axis=axis, keepdims=True) / 255.0
            s = jnp.maximum(s, 1e-08)
            q = jnp.clip(jnp.round(x / s), 0.0, 255.0) * s
            return x + jax.lax.stop_gradient(q - x)
        B, N, C = x.shape
        H, hd = (NUM_HEADS, HEAD_DIM)
        q = (x @ Wq + bq).reshape(1, B * N, H, hd)
        kv = (cond @ Wkv + bkv).reshape(1, -1, 2, H, hd)
        k, v = (kv[:, :, 0], kv[:, :, 1])
        scale = 1.0 / np.sqrt(hd).astype(np.float32)
        q = jnp.transpose(q * scale, (0, 2, 1, 3))
        k = jnp.transpose(k, (0, 2, 1, 3))
        v = jnp.transpose(v, (0, 2, 1, 3))
        q = _fq_sym(q, axis=-1)
        k = _fq_sym(k, axis=-1)
        v = _fq_sym(v, axis=2)
        attn = jnp.einsum('bhqd,bhkd->bhqk', q, k)
        attn = jax.nn.softmax(attn.astype(jnp.float32), axis=-1)
        attn = _fq_unsigned(attn, axis=-1)
        out = jnp.einsum('bhqk,bhkd->bhqd', attn, v)
        out = jnp.transpose(out, (0, 2, 1, 3)).reshape(B, N, C)
        return out @ Wp + bp

    def _L0_ffn_ref(hidden_states, gate_w, w_gate_up, w_down, shared_gate_up, shared_down):
        import jax, jax.numpy as jnp
        import numpy as np
        H = 256
        I = 176
        E = 16
        K = 2
        SI = I * 2

        def _swiglu(gu, inter):
            g, u = (gu[..., :inter], gu[..., inter:])
            return jax.nn.silu(g) * u
        orig_shape = hidden_states.shape
        x = hidden_states.reshape(-1, H)
        logits = jnp.einsum('th,eh->te', x, gate_w)
        scores = jax.nn.softmax(logits, axis=-1)
        topk_w, topk_idx = jax.lax.top_k(scores, K)
        combine = jnp.sum(jax.nn.one_hot(topk_idx, E, dtype=x.dtype) * topk_w[..., None], axis=1)
        gu = jnp.einsum('th,ehj->etj', x, w_gate_up)
        h = _swiglu(gu, I)
        y = jnp.einsum('eti,eih,te->th', h, w_down, combine)
        gu_s = x @ shared_gate_up
        y = y + _swiglu(gu_s, SI) @ shared_down
        return y.reshape(orig_shape)
    x = x + _L0_xattn_ref(_layernorm(x, axis=-1), ctx_2048, L0_xattn_Wq, L0_xattn_bq, L0_xattn_Wkv, L0_xattn_bkv, L0_xattn_Wp, L0_xattn_bp)
    x = x + _L0_ffn_ref(_layernorm(x, axis=-1), L0_ffn_gate_w, L0_ffn_w_gate_up, L0_ffn_w_down, L0_ffn_shared_gate_up, L0_ffn_shared_down)
    return x

_drawn_inputs = setup_inputs


def setup_inputs(seed=0):
    import zlib

    import numpy as np

    out = dict(_drawn_inputs(seed))
    spreads = {'L0_xattn_bq': (0.0, 0.8), 'L0_xattn_bkv': (0.0, 0.1), 'L0_xattn_bp': (0.0, 0.1)}
    factors = {'ctx_2048': 4.175,
     'L0_xattn_Wq': 8.0,
     'L0_xattn_Wkv': 4.388,
     'L0_ffn_gate_w': 8.0,
     'L0_ffn_w_gate_up': 8.0,
     'L0_ffn_w_down': 8.0,
     'L0_ffn_shared_gate_up': 2.859,
     'L0_ffn_shared_down': 2.859}
    for name, (base, spread) in spreads.items():
        noise = np.random.default_rng([zlib.crc32(name.encode()), seed]).standard_normal(out[name].shape)
        drawn = base * np.exp(spread * noise) if base else spread * noise
        out[name] = jnp.asarray(drawn.astype(out[name].dtype))
    for name, factor in factors.items():
        out[name] = (out[name] * factor).astype(out[name].dtype)
    return out
```

```python
from contextlib import ExitStack

import numpy as np

import concourse.bass as bass
from concourse import mybir

F32, BF16, U8, U32 = mybir.dt.float32, mybir.dt.bfloat16, mybir.dt.uint8, mybir.dt.uint32
ACT = mybir.ActivationFunctionType
ALU = mybir.AluOpType
AX = mybir.AxisListType

P = 128
MAGIC = 12582912.0
LN255 = 5.541263545158426
FLOOR = 1e-8
LN_EPS = 1e-5
BANK = 512


class Chain:

    def __init__(self, eng, sem, marks):
        self.eng, self.sem, self.marks, self.n, self.steps = eng, sem, marks, 0, 0

    def then(self, ins, apart=False):
        ins.then_inc(self.sem, 1)
        self.n = self.n + 1
        self.steps += 1
        self.eng.wait_ge(self.sem, self.n)
        if apart:
            self.eng.sem_inc(self.marks, 1)

    def loop(self, count, steps, body):
        before = self.n
        with self.eng.Fori(0, count) as i:
            self.n, self.steps = i * steps + before, 0
            body(i)
            assert self.steps == steps, (self.steps, steps)
        self.n = before + count * steps


def build(nc, x, ctx, Wq, bq, Wkv, bkv, Wp, bp, gate_w, w_gu, w_dn, s_gu, s_dn, out):
    B, N, D = x.shape
    NQ = B * N
    NK = ctx.shape[0] * ctx.shape[1]
    E, _, I2 = w_gu.shape
    I = I2 // 2
    HALF = I // 2
    H, HD = 16, 16
    PAIRS = H // 2
    NT = -(-NQ // P)
    NQL = NQ - (NT - 1) * P
    CH = 2 * BANK
    NF = NK // CH
    TAIL = NK - NF * CH
    NC = NF + 1
    NB = 2 * NC
    WL = (NK - (NB - 1) * BANK) // 4
    PEEL, LT, LP = 6, 2, 4
    assert D == 256 and NC % 2 == 1 and TAIL > BANK and NK % 4 == 0 and NC > PEEL + 2
    VG = -(-NB // NT)
    VBLK = VG * NT
    NM = PAIRS * NT
    NX = E + 2

    xf = x.rearrange("b n d -> (b n) d")
    of = out.rearrange("b n d -> (b n) d")
    cf = ctx.rearrange("b m d -> (b m) d")
    Kd = nc.dram_tensor("k_parts", [PAIRS, P, NK], BF16, kind="Internal").ap()
    Vd = nc.dram_tensor("v_values", [PAIRS, P, NB, P], F32, kind="Internal").ap()
    Qd = nc.dram_tensor("q_parts", [PAIRS, P, NT, 2 * P], BF16, kind="Internal").ap()

    with ExitStack() as es:
        def sb(name, shape, dt):
            return es.enter_context(nc.sbuf_tensor(name, shape, dt))

        def sem(name):
            return es.enter_context(nc.semaphore(name))

        ARENA = max(2 * NK * 2, 92416)
        arena = sb("arena", [P, ARENA], U8)
        X = sb("X", [P, NT, D], F32)
        OA = sb("OA", [P, NT, D], F32)
        VB = sb("VB", [P, 2 * VBLK * P], BF16)
        VS = sb("VS", [P, max(VBLK * P, 4096)], F32)
        QP = sb("QP", [P, 2 * NT * 2 * P], BF16)
        R = [sb(f"R{i}", [P, CH], U8) for i in range(2)]
        TT = [sb(f"TT{i}", [P, CH // 4], F32) for i in range(2)]
        RB = [sb(f"RB{i}", [P, CH], BF16) for i in range(2)]
        identf = sb("identf", [P, P], F32)
        identb = sb("identb", [P, P], BF16)
        NSQ = sb("NSQ", [P, NT * H], F32)
        MV = sb("MV", [P, NT, 2], F32)
        SD = sb("SD", [P, NT], F32)
        RSTD = sb("RSTD", [P, NT], F32)
        stat = sb("stat", [P, 6], F32)
        MX = sb("MX", [P, NB], F32)
        ZC = sb("ZC", [P, 2 * NC], F32)
        BS = sb("BS", [P, 2, 2], F32)
        sm = sb("sm", [P, 8], F32)
        VT = sb("VT", [P, VG * P], F32)
        svb = sb("svb", [P, D], F32)
        rvb = sb("rvb", [P, D], F32)
        PS = es.enter_context(nc.psum_tensor("PS", [P, 8 * BANK], F32))

        def bank(b, n=1):
            return PS[:, b * BANK:(b + n) * BANK]

        class Area:

            def __init__(self, ap, size):
                self.ap, self.at, self.size = ap, 0, size

            def take(self, n, dt, width):
                a = self.ap[:, self.at:self.at + n * width]
                self.at += n * width
                assert self.at <= self.size, (self.at, self.size)
                return a if dt == U8 else a.bitcast(dt)

        a1 = Area(arena, ARENA)
        CX = [a1.take(4 * D, F32, 4) for _ in range(2)]
        CT = [a1.take(8 * P, F32, 4) for _ in range(2)]
        KB = a1.take(4 * D, F32, 4)
        KR = a1.take(4 * D, F32, 4)
        KDQ = [a1.take(4 * D, F32, 4) for _ in range(2)]
        KREST = a1.take(4 * D, F32, 4)
        VST = [a1.take(4 * D, F32, 4) for _ in range(2)]
        KN = [a1.take(4 * PAIRS * P, BF16, 2) for _ in range(2)]
        KO = [a1.take(PAIRS * BANK, BF16, 2) for _ in range(2)]
        WKV = a1.take(2 * 2 * D, F32, 4)
        BKV = a1.take(2 * D, F32, 4)
        KAM, KS, KRC = (a1.take(4 * H, F32, 4) for _ in range(3))
        VM, VJ = (a1.take(D, F32, 4) for _ in range(2))
        a0 = Area(VS[:, :].bitcast(U8), VS.shape[1] * 4)
        XN = a0.take(D, F32, 4)
        XNT = a0.take(D, F32, 4)
        QF = a0.take(D, F32, 4)
        WQ = a0.take(2 * D, F32, 4)
        BQ = a0.take(D, F32, 4)
        QN = a0.take(H * P, BF16, 2)
        QT = a0.take(H * P, BF16, 2)
        QAM, QRC = a0.take(H, F32, 4), a0.take(H, F32, 4)
        KT = arena[:, 0:2 * NK * 2].bitcast(BF16)
        a2 = Area(arena, ARENA)
        WG = a2.take(NX * 2 * I2, F32, 4)
        WD = a2.take(NX * 2 * D, F32, 4)
        WPS = a2.take(2 * D, F32, 4)
        BP = a2.take(D, F32, 4)
        a3 = Area(VS[:, :].bitcast(U8), VS.shape[1] * 4)
        FA = a3.take(D, F32, 4)
        FT = a3.take(D, F32, 4)
        GWN = a3.take(D, F32, 4)
        GWT = a3.take(2 * E, F32, 4)
        SG = [a3.take(I, F32, 4) for _ in range(2)]
        HN = [a3.take(I, F32, 4) for _ in range(2)]
        HS = [a3.take(2 * P, F32, 4) for _ in range(2)]
        LG, SC, IO, OH = (a3.take(E, F32, 4) for _ in range(4))
        T8, I8F = a3.take(8, F32, 4), a3.take(8, F32, 4)
        I8 = a3.take(8, U32, 4)
        CB = a3.take(NT * NX, F32, 4)
        YO = a3.take(D, F32, 4)

        marks = sem("marks")
        consts, vchain, pchain, gchain = sem("consts"), sem("vchain"), sem("pchain"), sem("gchain")
        x_in, wq_in, wkv_in = sem("x_in"), sem("wq_in"), sem("wkv_in")
        var_ok, sd_ok = sem("var_ok"), sem("sd_ok")
        xn_ok, xt_ok, xtc_ok, q_ok, qn_ok, qt_ok, qtc_ok, q_out = (
            sem(n) for n in ("xn_ok", "xt_ok", "xtc_ok", "q_ok", "qn_ok", "qt_ok", "qtc_ok", "q_out"))
        cx_in = [sem(f"cx_in{i}") for i in range(2)]
        ct_ok, ctc_ok, kv_ok, kv_used, kd_ok, kn_ok, kt_ok, ktc_ok, v_ok = (
            sem(n) for n in ("ct_ok", "ctc_ok", "kv_ok", "kv_used", "kd_ok", "kn_ok", "kt_ok", "ktc_ok", "v_ok"))
        k_out, v_out = ([sem(f"{n}{i}") for i in range(2)] for n in ("k_out", "v_out"))
        vm_ok, vmx_ok = sem("vm_ok"), sem("vmx_ok")
        kq_in, vs_in, vs_zero, vq_ok = sem("kq_in"), sem("vs_in"), sem("vs_zero"), sem("vq_ok")
        a_ok, a_used, b_ok, r_ok, t_ok, tt_ok, rb_ok, pv_ok, o_ok, o_used, bias_ok = (
            sem(n) for n in ("a_ok", "a_used", "b_ok", "r_ok", "t_ok", "tt_ok", "rb_ok", "pv_ok", "o_ok", "o_used",
                             "bias_ok"))
        f_in, w_in, gw_ok, fa_ok, ft_ok, ftc_ok, fm_ok, fx_ok = (
            sem(n) for n in ("f_in", "w_in", "gw_ok", "fa_ok", "ft_ok", "ftc_ok", "fm_ok", "fx_ok"))
        lm_ok, le_ok, xs_ok, gu_ok, sg_ok, hn_ok, ht_ok, hs_ok, dn_ok, y_ok, yo_ok, y_out = (
            sem(n) for n in ("lm_ok", "le_ok", "xs_ok", "gu_ok", "sg_ok", "hn_ok", "ht_ok", "hs_ok", "dn_ok", "y_ok",
                             "yo_ok", "y_out"))
        block = es.enter_context(nc.Block())

        def of_round(m):
            return m // NT, m % NT

        def next_round(m):
            p, t = of_round(m + 1)
            return p % PAIRS, t

        def apart(eng):
            eng.sem_inc(marks, 1)

        def width(c):
            return CH if c < NC - 1 else TAIL

        def steps_of_item(eng, step):
            for c in range(PEEL):
                step(c, c % 2, c)
            with eng.Fori(0, (NC - 1 - PEEL) // 2) as k:
                c = k * 2 + PEEL
                step(c, 0, PEEL)
                step(c + 1, 1, PEEL + 1)
            step(NC - 1, 0, NC - 1)

        @block.sync
        def _(sp):
            full = (NT - 1) * P
            sp.dma_start(X[:, 0:NT - 1, :], xf[0:full, :].rearrange("(t q) d -> q t d", q=P)).then_inc(x_in, 16)
            sp.wait_ge(consts, 1)
            sp.dma_start(X[0:NQL, NT - 1, :], xf[full:NQ, :]).then_inc(x_in, 16)
            sp.dma_start(WQ.rearrange("p (c n) -> p c n", c=2), Wq.rearrange("(c p) n -> p c n", p=P)).then_inc(wq_in, 16)
            sp.dma_start(BQ, bq.partition_broadcast(P)).then_inc(wq_in, 16)
            sp.dma_start(WKV.rearrange("p (c n) -> p c n", c=2), Wkv.rearrange("(c p) n -> p c n", p=P)).then_inc(wkv_in, 16)
            sp.dma_start(BKV, bkv.partition_broadcast(P)).then_inc(wkv_in, 16)

            def load_ctx(b, s):
                if not isinstance(b, int) or b >= 2:
                    sp.wait_ge(ct_ok, b - 1)
                if isinstance(b, int) and b == NB - 1:
                    sp.dma_start(CX[s][0:WL, :], cf[b * BANK:NK, :].rearrange("(w j) d -> w (j d)", j=4)).then_inc(cx_in[s], 16)
                else:
                    sp.dma_start(CX[s], cf[bass.ds(b * BANK, BANK), :].rearrange("(w j) d -> w (j d)", j=4)).then_inc(cx_in[s], 16)

            load_ctx(0, 0)
            load_ctx(1, 1)

            with sp.Fori(0, NT) as t:
                sp.wait_ge(qtc_ok, t * 2 + 2)
                sp.dma_start(Qd[:, :, bass.ds(t, 1), :].rearrange("p r t n -> r p (t n)"),
                             QT.rearrange("r (p n) -> r p n", p=PAIRS)).then_inc(q_out, 16)

            def store(b, s):
                last = isinstance(b, int) and b == NB - 1
                parts, n = (WL, 4 * WL) if last else (P, BANK)
                sp.wait_ge(v_ok, b + 1)
                sp.dma_start(Vd[:, 0:parts, bass.ds(b, 1), :].rearrange("p w b n -> w p (b n)"),
                             VST[s][0:parts, :].rearrange("w (p n) -> w p n", p=PAIRS)).then_inc(v_out[s], 16)
                sp.wait_ge(ktc_ok, (b + 1) * PAIRS)
                sp.dma_start(Kd[:, :, bass.ds(b * BANK, n)].rearrange("p r n -> r p n"),
                             KO[s].rearrange("r (p n) -> r p n", p=PAIRS)[:, :, 0:n]).then_inc(k_out[s], 16)

            with sp.Fori(0, (NB - 4) // 2) as b2:
                b = b2 * 2
                for s in range(2):
                    load_ctx(b + 2 + s, s)
                    store(b + s, s)
            for b in range(NB - 4, NB):
                if b + 2 < NB:
                    load_ctx(b + 2, b % 2)
                store(b, b % 2)
            for s in range(2):
                sp.wait_ge(k_out[s], NB // 2 * 16)
                sp.wait_ge(v_out[s], NB // 2 * 16)
            sp.wait_ge(q_out, NT * 16)
            sp.wait_ge(vs_zero, 1)
            sp.wait_ge(vmx_ok, 1)

            def load_keys(p):
                if not isinstance(p, int) or p >= 2:
                    sp.wait_ge(b_ok, (p - 1) * (2 * NT * NC))
                sp.dma_start(KT[:, bass.ds((p % 2) * NK, NK)],
                             Kd[bass.ds(p, 1), :, :].rearrange("a r n -> r (a n)")).then_inc(kq_in, 16)
                sp.dma_start(QP[:, bass.ds((p % 2) * (NT * 2 * P), NT * 2 * P)],
                             Qd[bass.ds(p, 1), :, :, :].rearrange("a r t n -> r (a t n)")).then_inc(kq_in, 16)
                sp.wait_ge(kq_in, p * 32 + 32)
                apart(sp)

            def load_values(p):
                sp.wait_ge(vq_ok, p * NT)
                sp.dma_start(VS[:, 0:(NB - 1) * P],
                             Vd[bass.ds(p, 1), :, 0:NB - 1, :].rearrange("a w b n -> w (a b n)")).then_inc(vs_in, 16)
                sp.dma_start(VS[0:WL, (NB - 1) * P:NB * P],
                             Vd[bass.ds(p, 1), 0:WL, NB - 1:NB, :].rearrange("a w b n -> w (a b n)")).then_inc(vs_in, 16)
                sp.wait_ge(vs_in, p * 32 + 32)
                apart(sp)

            load_keys(0)
            load_values(0)
            load_values(1)
            load_keys(1)
            with sp.Fori(2, PAIRS) as p:
                load_values(p)
                load_keys(p)

            sp.wait_ge(a_used, (2 * NM + 1) * NB)
            sp.wait_ge(b_ok, 2 * NM * NC)
            sp.wait_ge(vq_ok, (PAIRS + 1) * NT)
            sp.dma_start(WPS.rearrange("p (c n) -> p c n", c=2), Wp.rearrange("(c p) n -> p c n", p=P)).then_inc(f_in, 16)
            sp.dma_start(BP, bp.partition_broadcast(P)).then_inc(f_in, 16)
            sp.dma_start(GWN[0:E, :], gate_w).then_inc(f_in, 16)
            wg = WG.rearrange("p (e c n) -> p e c n", e=NX, c=2)
            wd = WD.rearrange("p (e c n) -> p e c n", e=NX, c=2)
            with sp.Fori(0, E) as e:
                sp.dma_start(WG[:, bass.ds(e * (2 * I2), 2 * I2)].rearrange("p (c n) -> p c n", c=2),
                             w_gu[bass.ds(e, 1), :, :].rearrange("a (c p) n -> p (a c) n", p=P)).then_inc(w_in, 16)
                sp.dma_start(WD[0:HALF, bass.ds(e * (2 * D), 2 * D)].rearrange("p (c n) -> p c n", c=2),
                             w_dn[bass.ds(e, 1), :, :].rearrange("a (c p) n -> p (a c) n", p=HALF)).then_inc(w_in, 16)
            for k in range(2):
                for g in range(2):
                    sp.dma_start(wg[:, E + k, :, g * I:g * I + I],
                                 s_gu[:, (2 * g + k) * I:(2 * g + k + 1) * I].rearrange("(c p) n -> p c n", p=P)).then_inc(w_in, 16)
                sp.dma_start(wd[0:HALF, E + k, :, :],
                             s_dn[k * I:k * I + I, :].rearrange("(c p) n -> p c n", p=HALF)).then_inc(w_in, 16)
            with sp.Fori(0, NT - 1) as t:
                sp.wait_ge(yo_ok, t + 1)
                sp.dma_start(of[bass.ds(t * P, P), :], YO).then_inc(y_out, 16)
            sp.wait_ge(yo_ok, NT)
            sp.dma_start(of[full:NQ, :], YO[0:NQL, :]).then_inc(y_out, 16)
            sp.wait_ge(y_out, NT * 16)

        @block.gpsimd
        def _(pool):
            g = Chain(pool, gchain, marks)
            g.then(pool.memset(X[:, NT - 1, :], 0.0))
            g.then(pool.memset(identf[:, :], 0.0))
            g.then(pool.memset(identb[:, :], 0.0))
            g.then(pool.memset(QN, 0.0))
            g.then(pool.memset(KN[0], 0.0))
            g.then(pool.memset(KN[1], 0.0))
            for m in (identf, identb):
                g.then(pool.affine_select(out=m[:, :], in_=m[:, :], compare_op=ALU.not_equal, fill=1.0, base=0,
                                          pattern=[[-1, P]], channel_multiplier=1))
            pool.sem_inc(consts, 1)

            def split(b, s):
                kn = KN[s].rearrange("w (n d) -> w n d", d=64)
                rest = KREST.rearrange("w (n d) -> w n d", d=HD)
                pool.wait_ge(kd_ok, b + 1)
                g.then(pool.tensor_tensor(rest, KDQ[s].rearrange("w (n d) -> w n d", d=HD), kn[:, :, 0:HD], ALU.subtract), apart=True)
                g.then(pool.tensor_scalar(kn[:, :, HD:2 * HD], rest, 1.0, 0.0, ALU.mult, ALU.add))
                pool.tensor_tensor(kn[:, :, 2 * HD:3 * HD], rest, kn[:, :, HD:2 * HD], ALU.subtract).then_inc(kn_ok, 1)
                pool.wait_ge(kn_ok, b + 1)

            before = g.n
            with pool.Fori(0, (NB) // 2) as b2:
                b = b2 * 2
                for s in range(2):
                    g.n = b * 2 + (before + 2 * s)
                    split(b + s, s)
            g.n = before + 2 * NB
            pool.wait_ge(vm_ok, 1)
            pool.partition_all_reduce(svb[:, :], VM, P, bass.bass_isa.ReduceOp.max).then_inc(vmx_ok, 1)

            def widen(g_, s):
                pool.wait_ge(tt_ok, g_ + 1)
                if not isinstance(g_, int) or g_ >= 2:
                    pool.wait_ge(pv_ok, g_ - 1)
                apart(pool)
                pool.tensor_scalar(RB[s][:, :].rearrange("w (b j q) -> w b j q", b=2, j=4),
                                   TT[s][:, :].bitcast(U8).rearrange("w (b q j) -> w b j q", b=2, j=4),
                                   1.0, 0.0, ALU.mult, ALU.add).then_inc(rb_ok, 1)

            widen(0, 0)
            widen(1, 1)
            with pool.Fori(0, (2 * NM * NC - 2) // 2) as g_2:
                g_ = g_2 * 2 + 2
                widen(g_, 0)
                widen(g_ + 1, 1)

            pool.wait_ge(vq_ok, (PAIRS + 1) * NT)
            pool.iota(IO, pattern=[[1, E]], base=0, channel_multiplier=0,
                      allow_small_or_imprecise_dtypes=True).then_inc(gw_ok, 1)

        @block.tensor
        def _(pe):
            pe.wait_ge(consts, 1)
            pe.wait_ge(wq_in, 32)
            with pe.Fori(0, NT) as t:
                pe.wait_ge(xn_ok, t + 1)
                pe.wait_ge(qtc_ok, t * 2)
                for c in range(2):
                    last = nc.tensor.transpose(bank(6)[:, c * P:c * P + P], XN[:, c * P:c * P + P], identf[:, :])
                last.then_inc(xt_ok, 1)
                pe.wait_ge(xtc_ok, t + 1)
                for c in range(2):
                    last = nc.tensor.matmul(bank(7)[:, 0:D], XNT[:, c * P:c * P + P], WQ[:, c * D:c * D + D],
                                            start=c == 0, stop=c == 1)
                last.then_inc(q_ok, 1)
                pe.wait_ge(qn_ok, t + 1)
                for k in range(2):
                    for h in range(8):
                        last = nc.tensor.transpose(bank(6 + k).bitcast(BF16)[:, h * P:h * P + P],
                                                   QN[:, (8 * k + h) * P:(8 * k + h + 1) * P], identb[:, :])
                    last.then_inc(qt_ok, 1)

            def turn(b, s):
                pe.wait_ge(cx_in[s], (b // 2) * 16 + 16)
                if not isinstance(b, int) or b >= 1:
                    pe.wait_ge(ctc_ok, b)
                for j in range(4):
                    for c in range(2):
                        n = 2 * j + c
                        last = nc.tensor.transpose(bank(0, 2)[:, n * P:n * P + P],
                                                   CX[s][:, j * D + c * P:j * D + c * P + P], identf[:, :])
                last.then_inc(ct_ok, 1)

            def project(b, s):
                pe.wait_ge(ctc_ok, b + 1)
                for j in range(4):
                    if not isinstance(b, int) or b > 0 or j >= 2:
                        pe.wait_ge(kv_used, b * 4 + (j - 1))
                    for c in range(2):
                        n = 2 * j + c
                        last = nc.tensor.matmul(bank(2 + j % 2), CT[s][:, n * P:n * P + P], WKV[:, c * 2 * D:(c + 1) * 2 * D],
                                                start=c == 0, stop=c == 1)
                    last.then_inc(kv_ok, 1)

            def turn_keys(b, s):
                pe.wait_ge(kn_ok, b + 1)
                for p in range(PAIRS):
                    if not isinstance(b, int) or b > 0 or p >= 2:
                        pe.wait_ge(ktc_ok, b * PAIRS + (p - 1))
                    for j in range(4):
                        last = nc.tensor.transpose(bank(4 + p % 2).bitcast(BF16)[:, j * P:j * P + P],
                                                   KN[s][:, (j * PAIRS + p) * P:(j * PAIRS + p + 1) * P], identb[:, :])
                    last.then_inc(kt_ok, 1)

            pe.wait_ge(wkv_in, 32)
            turn(0, 0)
            turn(1, 1)
            project(0, 0)
            turn(2, 0)
            project(1, 1)
            turn_keys(0, 0)
            with pe.Fori(0, (NB - 2 - 2) // 2) as b2:
                b = b2 * 2 + 2
                for s in range(2):
                    turn(b + (s + 1), 1 - s)
                    project(b + s, s)
                    turn_keys(b + (s - 1), 1 - s)
            turn(NB - 1, 1)
            project(NB - 2, 0)
            turn_keys(NB - 3, 1)
            project(NB - 1, 1)
            turn_keys(NB - 2, 0)
            turn_keys(NB - 1, 1)

            def maxima(g, kq, c, cs, half):
                kb, qb = kq
                n = BANK if (cs < NC - 1 or half == 0) else TAIL - BANK
                if not isinstance(g, int) or g >= 1:
                    pe.wait_ge(a_used, g * 2 + (half - 1))
                nc.tensor.matmul(bank(4 + half)[:, 0:n], QP[:, bass.ds(qb, P)],
                                 KT[:, bass.ds(kb + (c * CH + half * BANK), n)], start=True, stop=True).then_inc(a_ok, 1)

            def scores(g, kq, c, cs, s):
                kb, qb = kq
                if not isinstance(g, int) or g >= 2:
                    pe.wait_ge(r_ok, g - 1)
                for half in range(2):
                    n = BANK if (cs < NC - 1 or half == 0) else TAIL - BANK
                    last = nc.tensor.matmul(bank(2 * s + half)[:, 0:n], QP[:, bass.ds(qb, P)],
                                            KT[:, bass.ds(kb + (c * CH + half * BANK), n)], start=True, stop=True)
                last.then_inc(b_ok, 1)

            def turn_bytes(g, s):
                pe.wait_ge(r_ok, g + 1)
                if not isinstance(g, int) or g >= 1:
                    pe.wait_ge(tt_ok, g)
                for b in range(2):
                    last = nc.tensor.transpose(bank(6)[:, b * P:b * P + P],
                                               R[s][:, b * BANK:b * BANK + BANK].bitcast(F32), identf[:, :])
                last.then_inc(t_ok, 1)

            def values(g, s, c, cs, vb, item, pair):
                pe.wait_ge(rb_ok, g + 1)
                if cs == 0:
                    pe.wait_ge(vq_ok, pair * NT + NT)
                    if not isinstance(item, int) or item >= 1:
                        pe.wait_ge(o_used, item)
                for n in range(8):
                    last = nc.tensor.matmul(bank(7)[:, 0:HD], RB[s][:, n * P:n * P + P],
                                            VB[:, bass.ds(vb + (c * (8 * 32) + n * 32), HD)],
                                            start=cs == 0 and n == 0, stop=cs == NC - 1 and n == 7)
                last.then_inc(pv_ok, 1)

            def keys_at(p, t, hh):
                return ((p % 2) * NK, (p % 2) * (NT * 2 * P) + t * (2 * P) + hh * P)

            def snap(v):
                return v if isinstance(v, int) else pe.snap(v)

            def values_at(p, hh):
                return (p % 2) * (VBLK * P) + hh * HD

            def round_(m):
                p, t = of_round(m)
                pn, tn = next_round(m)
                kb, qb = keys_at(p, t, 0)
                kb, qb0 = snap(kb), snap(qb)
                kbn, qbn = keys_at(pn, tn, 0)
                kbn, qbn = snap(kbn), snap(qbn)
                vb = snap(values_at(p, 0))
                first = isinstance(m, int) and m == 0
                vbp = None if first else snap(values_at(of_round(m - 1)[0], 1))
                pair = snap(p)
                for hh in range(2):
                    now = (kb, qb0 + hh * P)
                    ahead = (kb, qb0 + P) if hh == 0 else (kbn, qbn)
                    g0 = snap(m * (2 * NC) + hh * NC)
                    item = m * 2 + hh
                    if hh == 1:
                        pe.wait_ge(kq_in, pn * 32 + 32)

                    def step(c, par, cs):
                        g = g0 + c
                        s = (par + hh) % 2
                        if not (first and hh == 0 and cs < LT):
                            turn_bytes(g - LT, s)
                        scores(g, now, c, cs, s)
                        maxima(g + NC, ahead, c, cs, 0)
                        if cs >= LP:
                            values(g - LP, s, c - LP, cs - LP, vb + hh * HD, item, pair)
                        elif not (first and hh == 0):
                            values(g - LP, s, cs - LP + NC, cs - LP + NC, vbp if hh == 0 else vb, item - 1, pair)
                        maxima(g + NC, ahead, c, cs, 1)

                    steps_of_item(pe, step)

            pe.wait_ge(vm_ok, 1)
            pe.wait_ge(ktc_ok, NB * PAIRS)
            pe.wait_ge(qtc_ok, 2 * NT)
            pe.wait_ge(kq_in, 32)
            with pe.Fori(0, NC - 1) as c:
                for half in range(2):
                    pe.wait_ge(a_used, c * 2)
                    nc.tensor.matmul(bank(4 + half), QP[:, 0:P], KT[:, bass.ds(c * CH + half * BANK, BANK)],
                                     start=True, stop=True).then_inc(a_ok, 1)
            for half in range(2):
                maxima(NC - 1, (0, 0), NC - 1, NC - 1, half)
            round_(0)
            with pe.Fori(1, NM) as m:
                round_(m)
            g = 2 * NM * NC
            vb = values_at(PAIRS - 1, 1)
            for k in range(LP):
                if k < LT:
                    turn_bytes(g - LT + k, (g - LT + k) % 2)
                values(g - LP + k, (g - LP + k) % 2, NC - LP + k, NC - LP + k, vb, 2 * NM - 1, PAIRS - 1)

            pe.wait_ge(f_in, 48)
            pe.wait_ge(tt_ok, g)
            for c in range(2):
                last = nc.tensor.transpose(bank(0)[:, c * E:c * E + E], GWN[0:E, c * P:c * P + P], identf[0:E, 0:E])
            last.then_inc(ft_ok, 1)
            pe.wait_ge(ftc_ok, 1)
            with pe.Fori(0, NT) as t:
                pe.wait_ge(fa_ok, t + 1)
                for c in range(2):
                    last = nc.tensor.transpose(bank(0)[:, c * P:c * P + P], FA[:, c * P:c * P + P], identf[:, :])
                last.then_inc(ft_ok, 1)
                pe.wait_ge(ftc_ok, t + 2)
                for c in range(2):
                    last = nc.tensor.matmul(bank(1)[:, 0:D], FT[:, c * P:c * P + P], WPS[:, c * D:c * D + D],
                                            start=c == 0, stop=c == 1)
                last.then_inc(fm_ok, 1)
            with pe.Fori(0, NT) as t:
                pe.wait_ge(fa_ok, t + (NT + 1))
                for c in range(2):
                    last = nc.tensor.transpose(bank(0)[:, c * P:c * P + P], FA[:, c * P:c * P + P], identf[:, :])
                last.then_inc(ft_ok, 1)
                pe.wait_ge(ftc_ok, t + (NT + 2))
                for c in range(2):
                    last = nc.tensor.matmul(bank(1)[:, 0:E], FT[:, c * P:c * P + P], GWT[:, c * E:c * E + E],
                                            start=c == 0, stop=c == 1)
                last.then_inc(fm_ok, 1)
            pe.wait_ge(w_in, (2 * E + 6) * 16)

            def up(t, e, s, es_):
                n = t * NX + e
                if es_ >= 2:
                    pe.wait_ge(hn_ok, n - 1)
                elif not isinstance(t, int):
                    pe.wait_ge(hn_ok, t * NX)
                for c in range(2):
                    last = nc.tensor.matmul(bank(s)[:, 0:I2], FT[:, c * P:c * P + P],
                                            WG[:, bass.ds(e * (2 * I2) + c * I2, I2)], start=c == 0, stop=c == 1)
                last.then_inc(gu_ok, 1)

            def turn_hidden(t, e, s, es_):
                n = t * NX + e
                pe.wait_ge(hn_ok, n + 1)
                for c in range(2):
                    last = nc.tensor.transpose(bank(2 + s)[0:HALF, c * P:c * P + P], HN[s][:, c * HALF:(c + 1) * HALF],
                                               identf[:, :])
                last.then_inc(ht_ok, 1)

            def down(t, e, s, es_):
                n = t * NX + e
                pe.wait_ge(hs_ok, n + 1)
                for c in range(2):
                    last = nc.tensor.matmul(bank(4)[:, 0:D], HS[s][0:HALF, c * P:c * P + P],
                                            WD[0:HALF, bass.ds(e * (2 * D) + c * D, D)],
                                            start=es_ == 0 and c == 0, stop=es_ == NX - 1 and c == 1)
                last.then_inc(dn_ok, 1)

            with pe.Fori(0, NT) as t:
                pe.wait_ge(xs_ok, t + 1)
                pe.wait_ge(yo_ok, t)
                up(t, 0, 0, 0)
                up(t, 1, 1, 1)
                turn_hidden(t, 0, 0, 0)
                up(t, 2, 0, 2)
                turn_hidden(t, 1, 1, 1)
                down(t, 0, 0, 0)
                up(t, 3, 1, 3)
                turn_hidden(t, 2, 0, 2)
                down(t, 1, 1, 1)
                with pe.Fori(0, (NX - 4) // 2) as e2:
                    e = e2 * 2 + 4
                    for s in range(2):
                        up(t, e + s, s, 4)
                        turn_hidden(t, e + (s - 1), 1 - s, 3)
                        down(t, e + (s - 2), s, 2)
                turn_hidden(t, NX - 1, 1, NX - 1)
                down(t, NX - 2, 0, NX - 2)
                down(t, NX - 1, 1, NX - 1)

        @block.scalar
        def _(act):
            act.wait_ge(var_ok, 1)
            nc.scalar.activation(SD[:, :], RSTD[:, :], ACT.Sqrt).then_inc(sd_ok, 1)
            with act.Fori(0, NT) as t:
                act.wait_ge(xt_ok, t + 1)
                nc.scalar.activation(XNT, bank(6)[:, 0:D], ACT.Copy).then_inc(xtc_ok, 1)
                act.wait_ge(q_out, t * 16)
                for k in range(2):
                    act.wait_ge(qt_ok, t * 2 + (k + 1))
                    nc.scalar.activation(QT[:, k * 8 * P:(k + 1) * 8 * P], bank(6 + k).bitcast(BF16), ACT.Copy).then_inc(qtc_ok, 1)

            def copy_ctx(b, s):
                act.wait_ge(ct_ok, b + 1)
                if not isinstance(b, int) or b >= 2:
                    act.wait_ge(kv_ok, (b - 1) * 4)
                nc.scalar.activation(CT[s], bank(0, 2), ACT.Copy).then_inc(ctc_ok, 1)

            def copy_keys(b, s):
                w = WL if isinstance(b, int) and b == NB - 1 else P
                if not isinstance(b, int) or b >= 2:
                    act.wait_ge(k_out[s], (b // 2) * 16)
                for p in range(PAIRS):
                    act.wait_ge(kt_ok, b * PAIRS + (p + 1))
                    nc.scalar.activation(
                        KO[s].rearrange("r (p w j) -> r p w j", p=PAIRS, j=4)[:, p, 0:w, :],
                        bank(4 + p % 2).bitcast(BF16)[:, 0:4 * P].rearrange("r (j w) -> r w j", j=4)[:, 0:w, :],
                        ACT.Copy).then_inc(ktc_ok, 1)

            copy_ctx(0, 0)
            copy_ctx(1, 1)
            copy_ctx(2, 0)
            copy_keys(0, 0)
            with act.Fori(0, (NB - 2 - 2) // 2) as b2:
                b = b2 * 2 + 2
                for s in range(2):
                    copy_ctx(b + (s + 1), 1 - s)
                    copy_keys(b + (s - 1), 1 - s)
            copy_ctx(NB - 1, 1)
            copy_keys(NB - 3, 1)
            copy_keys(NB - 2, 0)
            copy_keys(NB - 1, 1)

            def round_(m):
                for hh in range(2):
                    item = m * 2 + hh
                    act.wait_ge(bias_ok, item + 1)
                    if not (isinstance(m, int) and m == 0):
                        act.wait_ge(o_used, item - 1)

                    def step(c, par, cs):
                        g = item * NC + c
                        s = (par + hh) % 2
                        w = width(cs)
                        act.wait_ge(b_ok, g + 1)
                        if not (isinstance(m, int) and hh == 0 and cs < 2):
                            act.wait_ge(t_ok, g - 1)
                        nc.scalar.activation(R[s][:, 0:w], bank(2 * s, 2)[:, 0:w], ACT.Exp, bias=BS[:, hh, 0:1],
                                             scale=BS[:, hh, 1:2],
                                             accum_out=ZC[:, bass.ds(hh * NC + c, 1)]).then_inc(r_ok, 1)

                    steps_of_item(act, step)

            round_(0)
            with act.Fori(1, NM) as m:
                round_(m)

            act.wait_ge(ft_ok, 1)
            nc.scalar.activation(GWT, bank(0)[:, 0:2 * E], ACT.Copy).then_inc(ftc_ok, 1)
            with act.Fori(0, NT) as t:
                act.wait_ge(ft_ok, t + 2)
                nc.scalar.activation(FT, bank(0)[:, 0:D], ACT.Copy).then_inc(ftc_ok, 1)
            act.wait_ge(var_ok, 2)
            nc.scalar.activation(SD[:, :], RSTD[:, :], ACT.Sqrt).then_inc(sd_ok, 1)
            with act.Fori(0, NT) as t:
                act.wait_ge(ft_ok, t + (NT + 2))
                nc.scalar.activation(FT, bank(0)[:, 0:D], ACT.Copy).then_inc(ftc_ok, 1)
                nc.scalar.activation(OA[:, bass.ds(t, 1), :].rearrange("p a n -> p (a n)"), bank(0)[:, 0:D],
                                                       ACT.Copy).then_inc(fx_ok, 1)
                act.wait_ge(lm_ok, t + 1)
                nc.scalar.activation(SC, LG, ACT.Exp, bias=sm[:, 0:1], accum_out=sm[:, 1:2]).then_inc(le_ok, 1)

            def gate(t, e, s, es_):
                n = t * NX + e
                act.wait_ge(gu_ok, n + 1)
                act.wait_ge(hn_ok, n - 1) if es_ >= 2 else act.wait_ge(hn_ok, t * NX)
                nc.scalar.activation(SG[s], bank(s)[:, 0:I], ACT.Silu).then_inc(sg_ok, 1)

            def copy_hidden(t, e, s, es_):
                n = t * NX + e
                act.wait_ge(ht_ok, n + 1)
                act.wait_ge(dn_ok, n - 1) if es_ >= 2 else act.wait_ge(dn_ok, t * NX)
                nc.scalar.activation(HS[s][0:HALF, :], bank(2 + s)[0:HALF, 0:2 * P], ACT.Copy).then_inc(hs_ok, 1)

            with act.Fori(0, NT) as t:
                act.wait_ge(gu_ok, t * NX)
                act.wait_ge(fx_ok, NT)
                nc.scalar.activation(FT, OA[:, bass.ds(t, 1), :].rearrange("p a n -> p (a n)"), ACT.Copy).then_inc(xs_ok, 1)
                gate(t, 0, 0, 0)
                gate(t, 1, 1, 1)
                copy_hidden(t, 0, 0, 0)
                gate(t, 2, 0, 2)
                copy_hidden(t, 1, 1, 1)
                gate(t, 3, 1, 3)
                copy_hidden(t, 2, 0, 2)
                with act.Fori(0, (NX - 4) // 2) as e2:
                    e = e2 * 2 + 4
                    for s in range(2):
                        gate(t, e + s, s, 4)
                        copy_hidden(t, e + (s - 1), 1 - s, 3)
                copy_hidden(t, NX - 1, 1, NX - 1)

        @block.vector
        def _(dve):
            v = Chain(dve, vchain, marks)
            dve.wait_ge(x_in, 32)

            def statistics():
                for t in range(NT):
                    v.then(nc.vector.bn_stats(stat[:, :], X[:, t, :]))
                    v.then(nc.vector.bn_aggr(MV[:, t, :], stat[:, :]))

            statistics()
            v.then(nc.vector.tensor_scalar_add(RSTD[:, :], MV[:, :, 1], LN_EPS))
            dve.sem_inc(var_ok, 1)
            dve.wait_ge(sd_ok, 1)
            v.then(nc.vector.reciprocal(RSTD[:, :], SD[:, :]))
            dve.wait_ge(wq_in, 32)
            v.then(nc.vector.tensor_scalar_mul(BQ, BQ, HD ** -0.5))
            dve.wait_ge(consts, 1)

            def normed(dst, t):
                return nc.vector.tensor_scalar(dst, X[:, bass.ds(t, 1), :].rearrange("p a n -> p (a n)"),
                                               MV[:, bass.ds(t, 1), 0:1].rearrange("p a n -> p (a n)"),
                                               RSTD[:, bass.ds(t, 1)], ALU.subtract, ALU.mult)

            def quantise_queries(t):
                normed(XN, t).then_inc(xn_ok, 1)
                dve.wait_ge(q_ok, t + 1)
                v.then(nc.vector.scalar_tensor_tensor(out=QF, in0=bank(7)[:, 0:D], scalar=HD ** -0.5, in1=BQ,
                                                      op0=ALU.mult, op1=ALU.add))
                q3 = QF.rearrange("p (h d) -> p h d", d=HD)
                v.then(nc.vector.tensor_reduce(QAM, q3, axis=AX.X, op=ALU.max, apply_absolute_value=True))
                v.then(nc.vector.tensor_scalar(QAM, QAM, 1.0 / 127.0, FLOOR, ALU.mult, ALU.max))
                v.then(nc.vector.tensor_scalar_mul(NSQ[:, bass.ds(t * H, H)], QAM, -1.0))
                v.then(nc.vector.reciprocal(QRC, QAM))
                v.then(nc.vector.tensor_tensor(q3, q3, QRC.unsqueeze(2).to_broadcast([P, H, HD]), ALU.mult))
                src = QF.rearrange("p (a b d) -> p a b d", b=2, d=HD)
                for part in range(3):
                    dst = QN.rearrange("p (a n) -> p a n", a=PAIRS)
                    for hh in range(2):
                        at = hh * (P + 64) + part * HD
                        v.then(nc.vector.tensor_scalar(dst[:, :, at:at + HD], src[:, :, hh, :], MAGIC, -MAGIC,
                                                       ALU.add, ALU.add))
                dve.sem_inc(qn_ok, 1)

            v.loop(NT, 12, quantise_queries)

            v.then(nc.vector.memset(VM, 0.0))
            dve.wait_ge(wkv_in, 32)

            def quantise_keys(b, s):
                last = isinstance(b, int) and b == NB - 1
                w = WL if last else P
                vst = VST[s].rearrange("w (p j n) -> w p j n", p=PAIRS, j=4)
                if not isinstance(b, int) or b >= 2:
                    dve.wait_ge(v_out[s], (b // 2) * 16)
                for j in range(4):
                    dve.wait_ge(kv_ok, b * 4 + (j + 1))
                    kv = bank(2 + j % 2)
                    nc.vector.tensor_tensor(KB[:, j * D:(j + 1) * D], kv[:, 0:D], BKV[:, 0:D], ALU.add)
                    v.then(nc.vector.tensor_tensor(vst[0:w, :, j, :], kv[0:w, D:2 * D].rearrange("w (p n) -> w p n", p=PAIRS),
                                                   BKV[0:w, D:2 * D].rearrange("w (p n) -> w p n", p=PAIRS), ALU.add))
                    dve.sem_inc(kv_used, 1)
                dve.sem_inc(v_ok, 1)
                k3 = KB.rearrange("w (n d) -> w n d", d=HD)
                v.then(nc.vector.tensor_reduce(KAM, k3, axis=AX.X, op=ALU.max, apply_absolute_value=True))
                nc.vector.tensor_reduce(VJ[0:w, :].rearrange("w (p n) -> w p n", p=PAIRS),
                                        vst[0:w].rearrange("w p j n -> w p n j"), axis=AX.X, op=ALU.max,
                                        apply_absolute_value=True)
                v.then(nc.vector.tensor_scalar(KS, KAM, 1.0 / 127.0, FLOOR, ALU.mult, ALU.max))
                v.then(nc.vector.reciprocal(KRC, KS))
                v.then(nc.vector.tensor_tensor(VM[0:w, :], VM[0:w, :], VJ[0:w, :], ALU.max))
                kr = KR.rearrange("w (n d) -> w n d", d=HD)
                v.then(nc.vector.tensor_tensor(kr, k3, KRC.unsqueeze(2).to_broadcast([P, 4 * H, HD]), ALU.mult))
                v.then(nc.vector.tensor_scalar(KR, KR, MAGIC, -MAGIC, ALU.add, ALU.add))
                if not isinstance(b, int) or b >= 2:
                    dve.wait_ge(kn_ok, b - 1)
                    dve.wait_ge(kt_ok, (b - 1) * PAIRS)
                v.then(nc.vector.tensor_tensor(KDQ[s].rearrange("w (n d) -> w n d", d=HD), kr,
                                               KS.unsqueeze(2).to_broadcast([P, 4 * H, HD]), ALU.mult))
                nc.vector.tensor_copy(KN[s].rearrange("w (n d) -> w n d", d=64)[:, :, 0:HD],
                                      KDQ[s].rearrange("w (n d) -> w n d", d=HD)).then_inc(kd_ok, 1)

            per = 11
            for b in range(2):
                quantise_keys(b, b)
            before = v.n
            with dve.Fori(0, (NB - 2 - 2) // 2) as b2:
                b = b2 * 2 + 2
                for s in range(2):
                    v.n = (b - 2) * per + (before + s * per)
                    v.steps = 0
                    quantise_keys(b + s, s)
                    assert v.steps == per, v.steps
            v.n = before + (NB - 4) * per
            quantise_keys(NB - 2, 0)
            quantise_keys(NB - 1, 1)
            dve.wait_ge(qtc_ok, 2 * NT)
            dve.wait_ge(q_out, NT * 16)
            v.then(nc.vector.memset(VS[:, :], 0.0))
            dve.sem_inc(vs_zero, 1)
            dve.sem_inc(vm_ok, 1)
            dve.wait_ge(vmx_ok, 1)
            v.then(nc.vector.tensor_scalar(svb[:, :], svb[:, :], 1.0 / 127.0, FLOOR, ALU.mult, ALU.max))
            v.then(nc.vector.reciprocal(rvb[:, :], svb[:, :]))

            def quantise_values(p, t, pw):
                n = VG * P
                src = VS[:, bass.ds(t * n, n)].rearrange("w (j n) -> w j n", n=32)
                tmp = VT[:, 0:n]
                v.then(nc.vector.tensor_tensor(tmp.rearrange("w (j n) -> w j n", n=32), src,
                                               rvb[:, bass.ds(p * 32, 32)].unsqueeze(1).to_broadcast([P, VG * 4, 32]), ALU.mult))
                v.then(nc.vector.tensor_scalar(VB[:, bass.ds((pw % 2) * (VBLK * P) + t * n, n)], tmp, MAGIC, -MAGIC,
                                               ALU.add, ALU.add))
                dve.sem_inc(vq_ok, 1)

            dve.wait_ge(vs_in, 32)
            v.loop(NT, 2, lambda t: quantise_values(0, t, 0))

            def evacuate(g, s):
                dve.wait_ge(t_ok, g + 1)
                if not isinstance(g, int) or g >= 2:
                    dve.wait_ge(rb_ok, g - 1)
                nc.vector.tensor_copy(TT[s][:, :], bank(6)[:, 0:CH // 4]).then_inc(tt_ok, 1)

            def maximum(g, c, cs, half):
                n = BANK if (cs < NC - 1 or half == 0) else TAIL - BANK
                dve.wait_ge(a_ok, g * 2 + (half + 1))
                nc.vector.tensor_reduce(MX[:, bass.ds(c * 2 + half, 1)], bank(4 + half)[:, 0:n], axis=AX.X,
                                        op=ALU.max).then_inc(a_used, 1)

            def bias_of(item, p, t, hh):
                dve.wait_ge(a_used, item * NB + NB)
                nsq = NSQ[:, bass.ds(t * H + p * 2 + hh, 1)]
                v.then(nc.vector.tensor_reduce(sm[:, 2:3], MX[:, :], axis=AX.X, op=ALU.max))
                nc.vector.tensor_scalar_mul(BS[:, hh, 1:2], nsq, -1.0)
                v.then(nc.vector.tensor_scalar(BS[:, hh, 0:1], sm[:, 2:3], nsq, LN255, ALU.mult, ALU.add))
                dve.sem_inc(bias_ok, 1)

            def heads_out(item, p, t, hh):
                dve.wait_ge(pv_ok, item * NC + NC)
                dve.wait_ge(r_ok, item * NC + NC)
                v.then(nc.vector.reduce_sum(sm[:, 3:4], ZC[:, hh * NC:(hh + 1) * NC], axis=AX.X))
                v.then(nc.vector.reciprocal(sm[:, 4:5], sm[:, 3:4]))
                v.then(nc.vector.tensor_scalar_mul(OA[:, bass.ds(t, 1), bass.ds(p * 32 + hh * HD, HD)].rearrange("q a n -> q (a n)"),
                                                   bank(7)[:, 0:HD], sm[:, 4:5]))
                dve.sem_inc(o_used, 1)

            def round_(m):
                first = isinstance(m, int) and m == 0
                p, t = of_round(m)
                pn, tn = next_round(m)
                for hh in range(2):
                    item = m * 2 + hh
                    def step(c, par, cs):
                        g = item * NC + c
                        s = (par + hh) % 2
                        if not (first and hh == 0 and cs < LT):
                            evacuate(g - LT, s)
                        if cs == LP and not (first and hh == 0):
                            if hh == 1:
                                heads_out(item - 1, p, t, 0)
                            else:
                                pb_, tb_ = of_round(m - 1)
                                heads_out(item - 1, pb_, tb_, 1)
                        if cs == LP + 1 and hh == 0:
                            pv = of_round(m)[0] + 1
                            pc = pv % PAIRS
                            dve.wait_ge(vs_in, pc * 32 + 32)
                            dve.wait_ge(pv_ok, item * NC)
                            quantise_values(pc, t, pv)
                        maximum(g + NC, c, cs, 0)
                        maximum(g + NC, c, cs, 1)

                    steps_of_item(dve, step)
                    if hh == 0:
                        bias_of(item + 1, p, t, 1)
                    else:
                        bias_of(item + 1, pn, tn, 0)

            with dve.Fori(0, NC - 1) as c:
                for half in range(2):
                    maximum(c, c, 0, half)
            for half in range(2):
                maximum(NC - 1, NC - 1, NC - 1, half)
            bias_of(0, 0, 0, 0)
            round_(0)
            per_round = 2 + 2 * 2 + 2 * 3
            before = v.n
            with dve.Fori(1, NM) as m:
                v.n, v.steps = (m - 1) * per_round + before, 0
                round_(m)
                assert v.steps == per_round, v.steps
            v.n = before + (NM - 1) * per_round
            g = 2 * NM * NC
            for k in range(LT):
                evacuate(g - LT + k, (g - LT + k) % 2)
            heads_out(2 * NM - 1, PAIRS - 1, NT - 1, 1)

            dve.wait_ge(f_in, 48)

            def project_out(t):
                v.then(nc.vector.tensor_tensor(FA, OA[:, bass.ds(t, 1), :].rearrange("p a n -> p (a n)"), svb[:, :], ALU.mult))
                dve.sem_inc(fa_ok, 1)
                xt = X[:, bass.ds(t, 1), :].rearrange("p a n -> p (a n)")
                dve.wait_ge(fm_ok, t + 1)
                v.then(nc.vector.tensor_tensor(YO, bank(1)[:, 0:D], BP, ALU.add))
                v.then(nc.vector.tensor_tensor(xt, xt, YO, ALU.add))

            v.loop(NT, 3, project_out)
            statistics()
            v.then(nc.vector.tensor_scalar_add(RSTD[:, :], MV[:, :, 1], LN_EPS))
            dve.sem_inc(var_ok, 1)
            dve.wait_ge(sd_ok, 2)
            v.then(nc.vector.reciprocal(RSTD[:, :], SD[:, :]))
            v.then(nc.vector.memset(CB, 1.0))
            dve.wait_ge(gw_ok, 1)

            def route(t):
                v.then(normed(FA, t))
                dve.sem_inc(fa_ok, 1)
                dve.wait_ge(fm_ok, t + (NT + 1))
                v.then(nc.vector.tensor_copy(LG, bank(1)[:, 0:E]))
                v.then(nc.vector.tensor_reduce(sm[:, 0:1], LG, axis=AX.X, op=ALU.max, negate=True))
                dve.sem_inc(lm_ok, 1)
                dve.wait_ge(le_ok, t + 1)
                v.then(nc.vector.reciprocal(sm[:, 5:6], sm[:, 1:2]))
                v.then(nc.vector.tensor_scalar_mul(SC, SC, sm[:, 5:6]), apart=True)
                v.then(nc.vector.max(T8, SC), apart=True)
                v.then(nc.vector.max_index(I8, T8, SC))
                v.then(nc.vector.tensor_copy(I8F, I8))
                v.then(nc.vector.tensor_scalar(OH, IO, I8F[:, 0:1], T8[:, 0:1], ALU.is_equal, ALU.mult))
                v.then(nc.vector.tensor_scalar(LG, IO, I8F[:, 1:2], T8[:, 1:2], ALU.is_equal, ALU.mult))
                v.then(nc.vector.tensor_tensor(CB[:, bass.ds(t * NX, E)], OH, LG, ALU.add))

            v.loop(NT, 11, route)

            def hidden(t, e, s, es_):
                n = t * NX + e
                dve.wait_ge(sg_ok, n + 1)
                dve.wait_ge(ht_ok, n - 1) if es_ >= 2 else dve.wait_ge(ht_ok, t * NX)
                nc.vector.scalar_tensor_tensor(out=HN[s], in0=bank(s)[:, I:I2], scalar=CB[:, bass.ds(n, 1)], in1=SG[s],
                                               op0=ALU.mult, op1=ALU.mult).then_inc(hn_ok, 1)

            with dve.Fori(0, NT) as t:
                hidden(t, 0, 0, 0)
                hidden(t, 1, 1, 1)
                with dve.Fori(0, (NX - 2) // 2) as e2:
                    e = e2 * 2 + 2
                    for s in range(2):
                        hidden(t, e + s, s, 2)
                dve.wait_ge(dn_ok, t * NX + NX)
                dve.wait_ge(y_out, t * 16)
                nc.vector.tensor_tensor(YO, X[:, bass.ds(t, 1), :].rearrange("p a n -> p (a n)"), bank(4)[:, 0:D],
                                        ALU.add).then_inc(yo_ok, 1)


_INS = ["x", "ctx_2048", "L0_xattn_Wq", "L0_xattn_bq", "L0_xattn_Wkv", "L0_xattn_bkv", "L0_xattn_Wp", "L0_xattn_bp",
        "L0_ffn_gate_w", "L0_ffn_w_gate_up", "L0_ffn_w_down", "L0_ffn_shared_gate_up", "L0_ffn_shared_down"]


def kernel(**inputs):
    import concourse.bacc as bacc
    from concourse.bass_utils import run_bass_kernel_spmd as run

    nc = bacc.Bacc("TRN2", target_bir_lowering=False, num_devices=1)
    arrays, args = {}, []
    for name in _INS:
        a = np.ascontiguousarray(inputs[name])
        arrays[f"in_{name}"] = a
        args.append(nc.dram_tensor(f"in_{name}", a.shape, mybir.dt.from_np(a.dtype), kind="ExternalInput").ap())
    out = nc.dram_tensor("out_0", inputs["x"].shape, F32, kind="ExternalOutput").ap()
    build(nc, *args, out)
    r = run(nc, [arrays], core_ids=[0])
    return r.results[0]["out_0"]
```

```python
from contextlib import ExitStack

import numpy as np

import concourse.bass as bass
from concourse import mybir

F32, BF16, U8, U32 = mybir.dt.float32, mybir.dt.bfloat16, mybir.dt.uint8, mybir.dt.uint32
ACT = mybir.ActivationFunctionType
ALU = mybir.AluOpType
AX = mybir.AxisListType

P = 128
MAGIC = 12582912.0
LN255 = 5.541263545158426
FLOOR = 1e-8
LN_EPS = 1e-5
BANK = 512
KV_BANKS = (2, 3, 6, 7)


class Chain:

    def __init__(self, eng, sem, marks):
        self.eng, self.sem, self.marks, self.n, self.steps = eng, sem, marks, 0, 0

    def then(self, ins, apart=False):
        self.begin(ins)
        self.settle()
        if apart:
            self.eng.sem_inc(self.marks, 1)

    def begin(self, ins):
        ins.then_inc(self.sem, 1)
        self.n = self.n + 1
        self.steps += 1

    def settle(self):
        self.eng.wait_ge(self.sem, self.n)

    def loop(self, count, steps, body):
        before = self.n
        with self.eng.Fori(0, count) as i:
            self.n, self.steps = i * steps + before, 0
            body(i)
            assert self.steps == steps, (self.steps, steps)
        self.n = before + count * steps


def build(nc, x, ctx, Wq, bq, Wkv, bkv, Wp, bp, gate_w, w_gu, w_dn, s_gu, s_dn, out):
    B, N, D = x.shape
    NQ = B * N
    NK = ctx.shape[0] * ctx.shape[1]
    E, _, I2 = w_gu.shape
    I = I2 // 2
    HALF = I // 2
    H, HD = 16, 16
    PAIRS = H // 2
    NT = -(-NQ // P)
    NQL = NQ - (NT - 1) * P
    CH = 2 * BANK
    NF = NK // CH
    TAIL = NK - NF * CH
    NC = NF + 1
    NB = 2 * NC
    WL = (NK - (NB - 1) * BANK) // 4
    NEAR = 4
    LT, LP, LEAD = 2, 4, 2
    assert D == 256 and NC % 2 == 1 and TAIL > BANK and NK % 4 == 0 and NC > LP + LEAD + 2 and NT > 1
    VG = -(-NB // NT)
    VBLK = VG * NT
    NM = PAIRS * NT
    NX = E + 2

    xf = x.rearrange("b n d -> (b n) d")
    of = out.rearrange("b n d -> (b n) d")
    cf = ctx.rearrange("b m d -> (b m) d")
    Kd = nc.dram_tensor("k_parts", [PAIRS, P, NK], BF16, kind="Internal").ap()
    Vd = nc.dram_tensor("v_values", [PAIRS, P, NB, P], F32, kind="Internal").ap()
    Qd = nc.dram_tensor("q_parts", [PAIRS, P, NT, 2 * P], BF16, kind="Internal").ap()

    with ExitStack() as es:
        def sb(name, shape, dt):
            return es.enter_context(nc.sbuf_tensor(name, shape, dt))

        def sem(name):
            return es.enter_context(nc.semaphore(name))

        ARENA = max(2 * NK * 2, 92416)
        arena = sb("arena", [P, ARENA], U8)
        X = sb("X", [P, NT, D], F32)
        OA = sb("OA", [P, NT, D], F32)
        VB = sb("VB", [P, VBLK * P], BF16)
        VN = sb("VN", [P, VBLK * P], BF16)
        VS = sb("VS", [P, max(VBLK * P, 4096)], F32)
        QP = sb("QP", [P, 2 * NT * 2 * P], BF16)
        R = [sb(f"R{i}", [P, CH], U8) for i in range(2)]
        TT = [sb(f"TT{i}", [P, CH // 4], F32) for i in range(2)]
        RB = [sb(f"RB{i}", [P, CH], BF16) for i in range(2)]
        identf = sb("identf", [P, P], F32)
        identb = sb("identb", [P, P], BF16)
        NSQ = sb("NSQ", [P, NT * H], F32)
        MV = sb("MV", [P, NT, 2], F32)
        SD = sb("SD", [P, NT], F32)
        RSTD = sb("RSTD", [P, NT], F32)
        stat = sb("stat", [P, 6], F32)
        MX = sb("MX", [P, 2 * NB], F32)
        ZC = sb("ZC", [P, 2 * NC], F32)
        BS = sb("BS", [P, 2, 2], F32)
        sm = sb("sm", [P, 8], F32)
        VT = sb("VT", [P, VG * P], F32)
        svb = sb("svb", [P, D], F32)
        rvb = sb("rvb", [P, D], F32)
        PS = es.enter_context(nc.psum_tensor("PS", [P, 8 * BANK], F32))

        def bank(b, n=1):
            return PS[:, b * BANK:(b + n) * BANK]

        class Area:

            def __init__(self, ap, size):
                self.ap, self.at, self.size = ap, 0, size

            def take(self, n, dt, width):
                a = self.ap[:, self.at:self.at + n * width]
                self.at += n * width
                assert self.at <= self.size, (self.at, self.size)
                return a if dt == U8 else a.bitcast(dt)

        a1 = Area(arena, ARENA)
        CX = [a1.take(4 * D, F32, 4) for _ in range(2)]
        CT = [a1.take(8 * P, F32, 4) for _ in range(2)]
        KB = a1.take(4 * D, F32, 4)
        KR = a1.take(4 * D, F32, 4)
        KDQ = [a1.take(4 * D, F32, 4) for _ in range(2)]
        KREST = a1.take(4 * D, F32, 4)
        VST = [a1.take(4 * D, F32, 4) for _ in range(2)]
        KN = [a1.take(4 * PAIRS * P, BF16, 2) for _ in range(2)]
        KO = [a1.take(PAIRS * BANK, BF16, 2) for _ in range(2)]
        WKV = a1.take(2 * 2 * D, F32, 4)
        BKV = a1.take(2 * D, F32, 4)
        KAM, KS, KRC = (a1.take(4 * H, F32, 4) for _ in range(3))
        VM, VJ = (a1.take(D, F32, 4) for _ in range(2))
        a0 = Area(VS[:, :].bitcast(U8), VS.shape[1] * 4)
        XN = a0.take(D, F32, 4)
        XNT = a0.take(D, F32, 4)
        QF = a0.take(D, F32, 4)
        WQ = a0.take(2 * D, F32, 4)
        BQ = a0.take(D, F32, 4)
        QN = a0.take(H * P, BF16, 2)
        QT = a0.take(H * P, BF16, 2)
        QAM, QRC = a0.take(H, F32, 4), a0.take(H, F32, 4)
        KT = arena[:, 0:2 * NK * 2].bitcast(BF16)
        a2 = Area(arena, ARENA)
        WG = a2.take(NX * 2 * I2, F32, 4)
        WD = a2.take(NX * 2 * D, F32, 4)
        WPS = a2.take(2 * D, F32, 4)
        BP = a2.take(D, F32, 4)
        a3 = Area(VS[:, :].bitcast(U8), VS.shape[1] * 4)
        FA = a3.take(D, F32, 4)
        FT = a3.take(D, F32, 4)
        GWN = a3.take(D, F32, 4)
        GWT = a3.take(2 * E, F32, 4)
        SG = [a3.take(I, F32, 4) for _ in range(2)]
        HN = [a3.take(I, F32, 4) for _ in range(2)]
        HS = [a3.take(2 * P, F32, 4) for _ in range(2)]
        LG, SC, IO, OH = (a3.take(E, F32, 4) for _ in range(4))
        T8, I8F = a3.take(8, F32, 4), a3.take(8, F32, 4)
        I8 = a3.take(8, U32, 4)
        CB = a3.take(NT * NX, F32, 4)
        YO = a3.take(D, F32, 4)

        marks = sem("marks")
        consts, vchain, pchain, gchain = sem("consts"), sem("vchain"), sem("pchain"), sem("gchain")
        x_in, wq_in, wkv_in = sem("x_in"), sem("wq_in"), sem("wkv_in")
        var_ok, sd_ok = sem("var_ok"), sem("sd_ok")
        xn_ok, xt_ok, xtc_ok, q_ok, qn_ok, qt_ok, qtc_ok, q_out = (
            sem(n) for n in ("xn_ok", "xt_ok", "xtc_ok", "q_ok", "qn_ok", "qt_ok", "qtc_ok", "q_out"))
        cx_in = [sem(f"cx_in{i}") for i in range(2)]
        ct_ok, ctc_ok, kv_ok, kv_used, kd_ok, kn_ok, kt_ok, ktc_ok, v_ok = (
            sem(n) for n in ("ct_ok", "ctc_ok", "kv_ok", "kv_used", "kd_ok", "kn_ok", "kt_ok", "ktc_ok", "v_ok"))
        k_out, v_out = ([sem(f"{n}{i}") for i in range(2)] for n in ("k_out", "v_out"))
        vm_ok, vmx_ok = sem("vm_ok"), sem("vmx_ok")
        kq_in, vs_in, vs_zero, vq_ok, vb_ok = (sem(n) for n in ("kq_in", "vs_in", "vs_zero", "vq_ok", "vb_ok"))
        a_ok, a_used, b_ok, r_ok, t_ok, tt_ok, rb_ok, pv_ok, o_ok, o_used, bias_ok = (
            sem(n) for n in ("a_ok", "a_used", "b_ok", "r_ok", "t_ok", "tt_ok", "rb_ok", "pv_ok", "o_ok", "o_used",
                             "bias_ok"))
        f_in, w_in, gw_ok, fa_ok, ft_ok, ftc_ok, fm_ok, fx_ok = (
            sem(n) for n in ("f_in", "w_in", "gw_ok", "fa_ok", "ft_ok", "ftc_ok", "fm_ok", "fx_ok"))
        lm_ok, le_ok, xs_ok, gu_ok, sg_ok, hn_ok, ht_ok, hs_ok, dn_ok, y_ok, yo_ok, y_out = (
            sem(n) for n in ("lm_ok", "le_ok", "xs_ok", "gu_ok", "sg_ok", "hn_ok", "ht_ok", "hs_ok", "dn_ok", "y_ok",
                             "yo_ok", "y_out"))
        block = es.enter_context(nc.Block())

        def next_round(m):
            return (m + 1) // NT % PAIRS, (m + 1) % NT

        def all_rounds(eng, round_, begin, end):
            with eng.Fori(0, PAIRS) as p:
                begin(p)
                round_(p, 0)
                with eng.Fori(1, NT) as t:
                    round_(p, t)
                end(p)

        def nothing(p):
            pass

        def on_scalar(c):
            return c % 3 != 0

        def wait_above_zero(eng, sem_, value):
            if not isinstance(value, int) or value > 0:
                eng.wait_ge(sem_, value)

        def apart(eng):
            eng.sem_inc(marks, 1)

        def width(c):
            return CH if c < NC - 1 else TAIL

        @block.sync
        def _(sp):
            full = (NT - 1) * P
            sp.dma_start(X[:, 0:NT - 1, :], xf[0:full, :].rearrange("(t q) d -> q t d", q=P)).then_inc(x_in, 16)
            sp.wait_ge(consts, 1)
            sp.dma_start(X[0:NQL, NT - 1, :], xf[full:NQ, :]).then_inc(x_in, 16)
            sp.dma_start(WQ.rearrange("p (c n) -> p c n", c=2), Wq.rearrange("(c p) n -> p c n", p=P)).then_inc(wq_in, 16)
            sp.dma_start(BQ, bq.partition_broadcast(P)).then_inc(wq_in, 16)
            sp.dma_start(WKV.rearrange("p (c n) -> p c n", c=2), Wkv.rearrange("(c p) n -> p c n", p=P)).then_inc(wkv_in, 16)
            sp.dma_start(BKV, bkv.partition_broadcast(P)).then_inc(wkv_in, 16)

            def load_ctx(b, s):
                if not isinstance(b, int) or b >= 2:
                    sp.wait_ge(ct_ok, b - 1)
                if isinstance(b, int) and b == NB - 1:
                    sp.dma_start(CX[s][0:WL, :], cf[b * BANK:NK, :].rearrange("(w j) d -> w (j d)", j=4)).then_inc(cx_in[s], 16)
                else:
                    sp.dma_start(CX[s], cf[bass.ds(b * BANK, BANK), :].rearrange("(w j) d -> w (j d)", j=4)).then_inc(cx_in[s], 16)

            load_ctx(0, 0)
            load_ctx(1, 1)

            with sp.Fori(0, NT) as t:
                sp.wait_ge(qtc_ok, t * 2 + 2)
                sp.dma_start(Qd[:, :, bass.ds(t, 1), :].rearrange("p r t n -> r p (t n)"),
                             QT.rearrange("r (p n) -> r p n", p=PAIRS)).then_inc(q_out, 16)

            def store_values(b, s):
                parts = WL if isinstance(b, int) and b == NB - 1 else P
                sp.wait_ge(v_ok, b + 1)
                sp.dma_start(Vd[:, 0:parts, bass.ds(b, 1), :].rearrange("p w b n -> w p (b n)"),
                             VST[s][0:parts, :].rearrange("w (p n) -> w p n", p=PAIRS)).then_inc(v_out[s], 16)

            def store_keys(b, s):
                n = 4 * WL if isinstance(b, int) and b == NB - 1 else BANK
                sp.wait_ge(ktc_ok, (b + 1) * PAIRS)
                sp.dma_start(Kd[:, :, bass.ds(b * BANK, n)].rearrange("p r n -> r p n"),
                             KO[s].rearrange("r (p n) -> r p n", p=PAIRS)[:, :, 0:n]).then_inc(k_out[s], 16)

            for i in range(3):
                load_ctx(i + 2, i % 2)
                if i >= 1:
                    store_values(i - 1, (i - 1) % 2)
            with sp.Fori(0, (NB - 6) // 2) as i2:
                for s in (1, 0):
                    i = i2 * 2 + (4 - s)
                    load_ctx(i + 2, s)
                    store_values(i - 1, 1 - s)
                    store_keys(i - 3, 1 - s)
            for i in range(NB - 3, NB + 3):
                if i + 2 < NB:
                    load_ctx(i + 2, i % 2)
                if i <= NB:
                    store_values(i - 1, (i - 1) % 2)
                store_keys(i - 3, (i - 3) % 2)
            for s in range(2):
                sp.wait_ge(k_out[s], NB // 2 * 16)
                sp.wait_ge(v_out[s], NB // 2 * 16)
            sp.wait_ge(q_out, NT * 16)
            sp.wait_ge(vs_zero, 1)
            sp.wait_ge(vmx_ok, 1)

            def load_keys(p):
                if not isinstance(p, int) or p >= 2:
                    sp.wait_ge(b_ok, (p - 1) * (2 * NT * NC))
                sp.dma_start(KT[:, bass.ds((p % 2) * NK, NK)],
                             Kd[bass.ds(p, 1), :, :].rearrange("a r n -> r (a n)")).then_inc(kq_in, 16)
                sp.dma_start(QP[:, bass.ds((p % 2) * (NT * 2 * P), NT * 2 * P)],
                             Qd[bass.ds(p, 1), :, :, :].rearrange("a r t n -> r (a t n)")).then_inc(kq_in, 16)
                sp.wait_ge(kq_in, p * 32 + 32)
                apart(sp)

            def load_values(p):
                wait_above_zero(sp, vq_ok, p * (NT * VG))
                sp.dma_start(VS[:, 0:(NB - 1) * P],
                             Vd[bass.ds(p, 1), :, 0:NB - 1, :].rearrange("a w b n -> w (a b n)")).then_inc(vs_in, 16)
                sp.dma_start(VS[0:WL, (NB - 1) * P:NB * P],
                             Vd[bass.ds(p, 1), 0:WL, NB - 1:NB, :].rearrange("a w b n -> w (a b n)")).then_inc(vs_in, 16)
                sp.wait_ge(vs_in, p * 32 + 32)
                apart(sp)

            load_keys(0)
            load_values(0)
            load_values(1)
            load_keys(1)
            with sp.Fori(2, PAIRS) as p:
                load_values(p)
                load_keys(p)

            sp.wait_ge(a_used, (2 * NM + 1) * NB + 2 * LEAD)
            sp.wait_ge(b_ok, 2 * NM * NC)
            sp.wait_ge(vq_ok, (PAIRS + 1) * NT * VG)
            sp.dma_start(WPS.rearrange("p (c n) -> p c n", c=2), Wp.rearrange("(c p) n -> p c n", p=P)).then_inc(f_in, 16)
            sp.dma_start(BP, bp.partition_broadcast(P)).then_inc(f_in, 16)
            sp.dma_start(GWN[0:E, :], gate_w).then_inc(f_in, 16)
            wg = WG.rearrange("p (e c n) -> p e c n", e=NX, c=2)
            wd = WD.rearrange("p (e c n) -> p e c n", e=NX, c=2)
            with sp.Fori(0, E) as e:
                sp.dma_start(WG[:, bass.ds(e * (2 * I2), 2 * I2)].rearrange("p (c n) -> p c n", c=2),
                             w_gu[bass.ds(e, 1), :, :].rearrange("a (c p) n -> p (a c) n", p=P)).then_inc(w_in, 16)
                sp.dma_start(WD[0:HALF, bass.ds(e * (2 * D), 2 * D)].rearrange("p (c n) -> p c n", c=2),
                             w_dn[bass.ds(e, 1), :, :].rearrange("a (c p) n -> p (a c) n", p=HALF)).then_inc(w_in, 16)
            for k in range(2):
                for g in range(2):
                    sp.dma_start(wg[:, E + k, :, g * I:g * I + I],
                                 s_gu[:, (2 * g + k) * I:(2 * g + k + 1) * I].rearrange("(c p) n -> p c n", p=P)).then_inc(w_in, 16)
                sp.dma_start(wd[0:HALF, E + k, :, :],
                             s_dn[k * I:k * I + I, :].rearrange("(c p) n -> p c n", p=HALF)).then_inc(w_in, 16)
            with sp.Fori(0, NT - 1) as t:
                sp.wait_ge(yo_ok, t + 1)
                sp.dma_start(of[bass.ds(t * P, P), :], YO).then_inc(y_out, 16)
            sp.wait_ge(yo_ok, NT)
            sp.dma_start(of[full:NQ, :], YO[0:NQL, :]).then_inc(y_out, 16)
            sp.wait_ge(y_out, NT * 16)

        @block.gpsimd
        def _(pool):
            g = Chain(pool, gchain, marks)
            g.then(pool.memset(X[:, NT - 1, :], 0.0))
            g.then(pool.memset(identf[:, :], 0.0))
            g.then(pool.memset(identb[:, :], 0.0))
            g.then(pool.memset(QN, 0.0))
            g.then(pool.memset(KN[0], 0.0))
            g.then(pool.memset(KN[1], 0.0))
            for m in (identf, identb):
                g.then(pool.affine_select(out=m[:, :], in_=m[:, :], compare_op=ALU.not_equal, fill=1.0, base=0,
                                          pattern=[[-1, P]], channel_multiplier=1))
            pool.sem_inc(consts, 1)

            def split(b, s):
                kn = KN[s].rearrange("w (n d) -> w n d", d=64)
                rest = KREST.rearrange("w (n d) -> w n d", d=HD)
                pool.wait_ge(kd_ok, b + 1)
                g.then(pool.tensor_tensor(rest, KDQ[s].rearrange("w (n d) -> w n d", d=HD), kn[:, :, 0:HD], ALU.subtract), apart=True)
                g.then(pool.tensor_scalar(kn[:, :, HD:2 * HD], rest, 1.0, 0.0, ALU.mult, ALU.add))
                pool.tensor_tensor(kn[:, :, 2 * HD:3 * HD], rest, kn[:, :, HD:2 * HD], ALU.subtract).then_inc(kn_ok, 1)
                pool.wait_ge(kn_ok, b + 1)

            before = g.n
            with pool.Fori(0, (NB) // 2) as b2:
                b = b2 * 2
                for s in range(2):
                    g.n = b * 2 + (before + 2 * s)
                    split(b + s, s)
            g.n = before + 2 * NB
            pool.wait_ge(vm_ok, 1)
            pool.partition_all_reduce(svb[:, :], VM, P, bass.bass_isa.ReduceOp.max).then_inc(vmx_ok, 1)

            def widen(g_, s):
                pool.wait_ge(tt_ok, g_ + 1)
                if not isinstance(g_, int) or g_ >= 2:
                    pool.wait_ge(pv_ok, g_ - 1)
                apart(pool)
                pool.tensor_scalar(RB[s][:, :].rearrange("w (b j q) -> w b j q", b=2, j=4),
                                   TT[s][:, :].bitcast(U8).rearrange("w (b q j) -> w b j q", b=2, j=4),
                                   1.0, 0.0, ALU.mult, ALU.add).then_inc(rb_ok, 1)

            widen(0, 0)
            widen(1, 1)
            with pool.Fori(0, (2 * NM * NC - 2) // 2) as g_2:
                g_ = g_2 * 2 + 2
                widen(g_, 0)
                widen(g_ + 1, 1)

            pool.wait_ge(vq_ok, (PAIRS + 1) * NT * VG)
            pool.iota(IO, pattern=[[1, E]], base=0, channel_multiplier=0,
                      allow_small_or_imprecise_dtypes=True).then_inc(gw_ok, 1)

        @block.tensor
        def _(pe):
            pe.wait_ge(consts, 1)
            pe.wait_ge(wq_in, 32)
            def queries(t):
                pe.wait_ge(xn_ok, t + 1)
                wait_above_zero(pe, qtc_ok, t * 2)
                for c in range(2):
                    last = nc.tensor.transpose(bank(6)[:, c * P:c * P + P], XN[:, c * P:c * P + P], identf[:, :])
                last.then_inc(xt_ok, 1)
                pe.wait_ge(xtc_ok, t + 1)
                for c in range(2):
                    last = nc.tensor.matmul(bank(7)[:, 0:D], XNT[:, c * P:c * P + P], WQ[:, c * D:c * D + D],
                                            start=c == 0, stop=c == 1)
                last.then_inc(q_ok, 1)
                pe.wait_ge(qn_ok, t + 1)
                for k in range(2):
                    for h in range(8):
                        last = nc.tensor.transpose(bank(6 + k).bitcast(BF16)[:, h * P:h * P + P],
                                                   QN[:, (8 * k + h) * P:(8 * k + h + 1) * P], identb[:, :])
                    last.then_inc(qt_ok, 1)

            queries(0)
            with pe.Fori(1, NT) as t:
                queries(t)

            def turn(b, s):
                pe.wait_ge(cx_in[s], (b // 2) * 16 + 16)
                if not isinstance(b, int) or b >= 1:
                    pe.wait_ge(ctc_ok, b)
                for j in range(4):
                    for c in range(2):
                        n = 2 * j + c
                        last = nc.tensor.transpose(bank(0, 2)[:, n * P:n * P + P],
                                                   CX[s][:, j * D + c * P:j * D + c * P + P], identf[:, :])
                last.then_inc(ct_ok, 1)

            def project(b, s):
                pe.wait_ge(ctc_ok, b + 1)
                for j in range(4):
                    if not isinstance(b, int) or b > 0:
                        pe.wait_ge(kv_used, b * 4 + (j - 3))
                    for c in range(2):
                        n = 2 * j + c
                        last = nc.tensor.matmul(bank(KV_BANKS[j]), CT[s][:, n * P:n * P + P], WKV[:, c * 2 * D:(c + 1) * 2 * D],
                                                start=c == 0, stop=c == 1)
                    last.then_inc(kv_ok, 1)

            def turn_keys(b, s):
                pe.wait_ge(kn_ok, b + 1)
                for p in range(PAIRS):
                    if not isinstance(b, int) or b > 0 or p >= 2:
                        pe.wait_ge(ktc_ok, b * PAIRS + (p - 1))
                    for j in range(4):
                        last = nc.tensor.transpose(bank(4 + p % 2).bitcast(BF16)[:, j * P:j * P + P],
                                                   KN[s][:, (j * PAIRS + p) * P:(j * PAIRS + p + 1) * P], identb[:, :])
                    last.then_inc(kt_ok, 1)

            pe.wait_ge(wkv_in, 32)
            pe.wait_ge(qtc_ok, 2 * NT)
            turn(0, 0)
            turn(1, 1)
            project(0, 0)
            turn(2, 0)
            project(1, 1)

            def block_of_keys(b, s):
                turn(b + 1, 1 - s)
                project(b, s)
                turn_keys(b - 2, s)

            block_of_keys(2, 0)
            block_of_keys(3, 1)
            with pe.Fori(0, (NB - 6) // 2) as b2:
                b = b2 * 2 + 4
                for s in range(2):
                    block_of_keys(b + s, s)
            block_of_keys(NB - 2, 0)
            project(NB - 1, 1)
            for b in range(NB - 3, NB):
                turn_keys(b, b % 2)

            near_b, near_a = pe.alloc_register("keys_of_pass_b"), pe.alloc_register("keys_of_pass_a")

            def copy_of(register, value):
                pe.reg_mov(register, value)
                return pe.snap(register, min_val=0, max_val=NK)

            def maxima(g, kq, c, half):
                kb, qb = kq
                n = BANK if (c < NC - 1 or half == 0) else TAIL - BANK
                wait_above_zero(pe, a_used, g * 2 + (half - 1))
                nc.tensor.matmul(bank(4 + half)[:, 0:n], QP[:, bass.ds(qb, P)],
                                 KT[:, bass.ds(kb + (c * CH + half * BANK), n)], start=True, stop=True).then_inc(a_ok, 1)

            def scores(g, kq, c, s):
                kb, qb = kq
                for half in range(2):
                    n = BANK if (c < NC - 1 or half == 0) else TAIL - BANK
                    last = nc.tensor.matmul(bank(2 * s + half)[:, 0:n], QP[:, bass.ds(qb, P)],
                                            KT[:, bass.ds(kb + (c * CH + half * BANK), n)], start=True, stop=True)
                last.then_inc(b_ok, 1)

            def turn_bytes(g, s, fresh=False):
                pe.wait_ge(r_ok, g + 1)
                if not fresh:
                    pe.wait_ge(tt_ok, g)
                for b in range(2):
                    last = nc.tensor.transpose(bank(6)[:, b * P:b * P + P],
                                               R[s][:, b * BANK:b * BANK + BANK].bitcast(F32), identf[:, :])
                last.then_inc(t_ok, 1)

            def values(g, s, c, hh):
                pe.wait_ge(rb_ok, g + 1)
                for n in range(8):
                    at = (c * 8 + n) * 32 + hh * HD
                    last = nc.tensor.matmul(bank(7)[:, 0:HD], RB[s][:, n * P:n * P + P], VB[:, at:at + HD],
                                            start=c == 0 and n == 0, stop=c == NC - 1 and n == 7)
                last.then_inc(pv_ok, 1)

            def snap(v):
                return v if isinstance(v, int) else pe.snap(v)

            def keys_at(p, t):
                return snap((p % 2) * NK), snap((p % 2) * (NT * 2 * P) + t * (2 * P))

            def round_(p, t):
                m = p * NT + t
                pn, tn = next_round(m)
                first = isinstance(t, int) and t == 0
                kb, qb = keys_at(p, t)
                kbn, qbn = keys_at(pn, tn)
                kq = [(kb, qb), (kb, snap(qb + P)), (kbn, qbn), (kbn, snap(qbn + P))]
                for hh in range(2):
                    g0 = snap(m * (2 * NC) + hh * NC)
                    item = m * 2 + hh
                    fresh = first and hh == 0
                    for c in range(NC):
                        g, s = g0 + c, (c + hh) % 2
                        ka, qa = kq[hh + 1] if c < NC - LEAD else kq[hh + 2]
                        if c % NEAR == 0:
                            keys_b = copy_of(near_b, kb)
                        if c % NEAR == 0 or c == NC - LEAD:
                            keys_a = copy_of(near_a, ka) if ka is not kb else keys_b
                        if hh == 0 and c == NC - LEAD:
                            pe.wait_ge(kq_in, pn * 32 + 32)
                        if c >= LT or not fresh:
                            turn_bytes(g - LT, s, fresh and c == LT)
                        scores(g, (keys_b, kq[hh][1]), c, s)
                        maxima(g + (NC + LEAD), (keys_a, qa), c, 0)
                        if c >= LP:
                            if c == LP and fresh:
                                pe.wait_ge(vb_ok, p + 1)
                            elif c == LP:
                                pe.wait_ge(o_used, item)
                            values(g - LP, s, c - LP, hh)
                        elif not fresh:
                            values(g - LP, s, c - LP + NC, 1 - hh)
                        maxima(g + (NC + LEAD), (keys_a, qa), c, 1)

            def finish(p):
                g = (p + 1) * (2 * NT * NC)
                for k in range(LP):
                    if k < LT:
                        turn_bytes(g + (k - LT), k % 2)
                    values(g + (k - LP), k % 2, NC - LP + k, 1)

            pe.wait_ge(vm_ok, 1)
            pe.wait_ge(ktc_ok, NB * PAIRS)
            pe.wait_ge(qtc_ok, 2 * NT)
            pe.wait_ge(kq_in, 32)
            for half in range(2):
                maxima(0, (0, 0), 0, half)
            with pe.Fori(1, NC - 1) as c:
                for half in range(2):
                    pe.wait_ge(a_used, c * 2 + (half - 1))
                    nc.tensor.matmul(bank(4 + half), QP[:, 0:P], KT[:, bass.ds(c * CH + half * BANK, BANK)],
                                     start=True, stop=True).then_inc(a_ok, 1)
            for half in range(2):
                maxima(NC - 1, (0, 0), NC - 1, half)
            for c in range(NC - LEAD, NC):
                for half in range(2):
                    maxima(c + LEAD, (0, P), c, half)
            all_rounds(pe, round_, nothing, finish)

            pe.wait_ge(f_in, 48)
            pe.wait_ge(tt_ok, 2 * NM * NC)
            for c in range(2):
                last = nc.tensor.transpose(bank(0)[:, c * E:c * E + E], GWN[0:E, c * P:c * P + P], identf[0:E, 0:E])
            last.then_inc(ft_ok, 1)
            pe.wait_ge(ftc_ok, 1)
            with pe.Fori(0, NT) as t:
                pe.wait_ge(fa_ok, t + 1)
                for c in range(2):
                    last = nc.tensor.transpose(bank(0)[:, c * P:c * P + P], FA[:, c * P:c * P + P], identf[:, :])
                last.then_inc(ft_ok, 1)
                pe.wait_ge(ftc_ok, t + 2)
                for c in range(2):
                    last = nc.tensor.matmul(bank(1)[:, 0:D], FT[:, c * P:c * P + P], WPS[:, c * D:c * D + D],
                                            start=c == 0, stop=c == 1)
                last.then_inc(fm_ok, 1)
            with pe.Fori(0, NT) as t:
                pe.wait_ge(fa_ok, t + (NT + 1))
                for c in range(2):
                    last = nc.tensor.transpose(bank(0)[:, c * P:c * P + P], FA[:, c * P:c * P + P], identf[:, :])
                last.then_inc(ft_ok, 1)
                pe.wait_ge(ftc_ok, t + (NT + 2))
                for c in range(2):
                    last = nc.tensor.matmul(bank(1)[:, 0:E], FT[:, c * P:c * P + P], GWT[:, c * E:c * E + E],
                                            start=c == 0, stop=c == 1)
                last.then_inc(fm_ok, 1)
            pe.wait_ge(w_in, (2 * E + 6) * 16)

            def up(t, e, s, es_):
                n = t * NX + e
                wait_above_zero(pe, hn_ok, n - 1 if es_ >= 2 else t * NX)
                for c in range(2):
                    last = nc.tensor.matmul(bank(s)[:, 0:I2], FT[:, c * P:c * P + P],
                                            WG[:, bass.ds(e * (2 * I2) + c * I2, I2)], start=c == 0, stop=c == 1)
                last.then_inc(gu_ok, 1)

            def turn_hidden(t, e, s, es_):
                n = t * NX + e
                pe.wait_ge(hn_ok, n + 1)
                for c in range(2):
                    last = nc.tensor.transpose(bank(2 + s)[0:HALF, c * P:c * P + P], HN[s][:, c * HALF:(c + 1) * HALF],
                                               identf[:, :])
                last.then_inc(ht_ok, 1)

            def down(t, e, s, es_):
                n = t * NX + e
                pe.wait_ge(hs_ok, n + 1)
                for c in range(2):
                    last = nc.tensor.matmul(bank(4)[:, 0:D], HS[s][0:HALF, c * P:c * P + P],
                                            WD[0:HALF, bass.ds(e * (2 * D) + c * D, D)],
                                            start=es_ == 0 and c == 0, stop=es_ == NX - 1 and c == 1)
                last.then_inc(dn_ok, 1)

            def experts(t):
                pe.wait_ge(xs_ok, t + 1)
                wait_above_zero(pe, yo_ok, t)
                up(t, 0, 0, 0)
                up(t, 1, 1, 1)
                turn_hidden(t, 0, 0, 0)
                up(t, 2, 0, 2)
                turn_hidden(t, 1, 1, 1)
                down(t, 0, 0, 0)
                up(t, 3, 1, 3)
                turn_hidden(t, 2, 0, 2)
                down(t, 1, 1, 1)
                with pe.Fori(0, (NX - 4) // 2) as e2:
                    e = e2 * 2 + 4
                    for s in range(2):
                        up(t, e + s, s, 4)
                        turn_hidden(t, e + (s - 1), 1 - s, 3)
                        down(t, e + (s - 2), s, 2)
                turn_hidden(t, NX - 1, 1, NX - 1)
                down(t, NX - 2, 0, NX - 2)
                down(t, NX - 1, 1, NX - 1)

            experts(0)
            with pe.Fori(1, NT) as t:
                experts(t)

        @block.scalar
        def _(act):
            act.wait_ge(var_ok, 1)
            nc.scalar.activation(SD[:, :], RSTD[:, :], ACT.Sqrt).then_inc(sd_ok, 1)
            def copy_queries(t):
                act.wait_ge(xt_ok, t + 1)
                nc.scalar.activation(XNT, bank(6)[:, 0:D], ACT.Copy).then_inc(xtc_ok, 1)
                wait_above_zero(act, q_out, t * 16)
                for k in range(2):
                    act.wait_ge(qt_ok, t * 2 + (k + 1))
                    nc.scalar.activation(QT[:, k * 8 * P:(k + 1) * 8 * P], bank(6 + k).bitcast(BF16), ACT.Copy).then_inc(qtc_ok, 1)

            copy_queries(0)
            with act.Fori(1, NT) as t:
                copy_queries(t)

            def copy_ctx(b, s):
                act.wait_ge(ct_ok, b + 1)
                if not isinstance(b, int) or b >= 2:
                    act.wait_ge(kv_ok, (b - 1) * 4)
                nc.scalar.activation(CT[s], bank(0, 2), ACT.Copy).then_inc(ctc_ok, 1)

            def copy_keys(b, s):
                w = WL if isinstance(b, int) and b == NB - 1 else P
                if not isinstance(b, int) or b >= 2:
                    act.wait_ge(k_out[s], (b // 2) * 16)
                for p in range(PAIRS):
                    act.wait_ge(kt_ok, b * PAIRS + (p + 1))
                    nc.scalar.activation(
                        KO[s].rearrange("r (p w j) -> r p w j", p=PAIRS, j=4)[:, p, 0:w, :],
                        bank(4 + p % 2).bitcast(BF16)[:, 0:4 * P].rearrange("r (j w) -> r w j", j=4)[:, 0:w, :],
                        ACT.Copy).then_inc(ktc_ok, 1)

            for b in range(3):
                copy_ctx(b, b % 2)
            for b in (2, 3):
                copy_ctx(b + 1, 1 - b % 2)
                copy_keys(b - 2, b % 2)
            with act.Fori(0, (NB - 6) // 2) as b2:
                b = b2 * 2 + 4
                for s in range(2):
                    copy_ctx(b + (s + 1), 1 - s)
                    copy_keys(b + (s - 2), s)
            copy_ctx(NB - 1, 1)
            for b in range(NB - 4, NB):
                copy_keys(b, b % 2)

            def copy_bytes(g, s, fresh=False):
                act.wait_ge(t_ok, g + 1)
                if not fresh:
                    act.wait_ge(rb_ok, g - 1)
                nc.scalar.copy(TT[s][:, :], bank(6)[:, 0:CH // 4]).then_inc(tt_ok, 1)

            def round_(p, t):
                for hh in range(2):
                    item = (p * NT + t) * 2 + hh
                    fresh = isinstance(t, int) and t == 0 and hh == 0
                    act.wait_ge(bias_ok, item + 1)
                    g0 = act.snap(item * NC)
                    for c in range(NC):
                        g, s, w = g0 + c, (c + hh) % 2, width(c)
                        if on_scalar((c - LT) % NC) and not (fresh and c < LT):
                            copy_bytes(g - LT, s, fresh and c - LT < 2)
                        act.wait_ge(b_ok, g + 1)
                        nc.scalar.activation(R[s][:, 0:w], bank(2 * s, 2)[:, 0:w], ACT.Exp, bias=BS[:, hh, 0:1],
                                             scale=BS[:, hh, 1:2],
                                             accum_out=ZC[:, hh * NC + c:hh * NC + c + 1]).then_inc(r_ok, 1)

            def finish(p):
                g = (p + 1) * (2 * NT * NC)
                for k in range(LT):
                    if on_scalar(NC - LT + k):
                        copy_bytes(g + (k - LT), k % 2)

            all_rounds(act, round_, nothing, finish)

            act.wait_ge(ft_ok, 1)
            nc.scalar.activation(GWT, bank(0)[:, 0:2 * E], ACT.Copy).then_inc(ftc_ok, 1)
            with act.Fori(0, NT) as t:
                act.wait_ge(ft_ok, t + 2)
                nc.scalar.activation(FT, bank(0)[:, 0:D], ACT.Copy).then_inc(ftc_ok, 1)
            act.wait_ge(var_ok, 2)
            nc.scalar.activation(SD[:, :], RSTD[:, :], ACT.Sqrt).then_inc(sd_ok, 1)
            with act.Fori(0, NT) as t:
                act.wait_ge(ft_ok, t + (NT + 2))
                nc.scalar.activation(FT, bank(0)[:, 0:D], ACT.Copy).then_inc(ftc_ok, 1)
                nc.scalar.activation(OA[:, bass.ds(t, 1), :].rearrange("p a n -> p (a n)"), bank(0)[:, 0:D],
                                                       ACT.Copy).then_inc(fx_ok, 1)
                act.wait_ge(lm_ok, t + 1)
                nc.scalar.activation(SC, LG, ACT.Exp, bias=sm[:, 0:1], accum_out=sm[:, 1:2]).then_inc(le_ok, 1)

            def gate(t, e, s, es_):
                n = t * NX + e
                act.wait_ge(gu_ok, n + 1)
                wait_above_zero(act, hn_ok, n - 1 if es_ >= 2 else t * NX)
                nc.scalar.activation(SG[s], bank(s)[:, 0:I], ACT.Silu).then_inc(sg_ok, 1)

            def copy_hidden(t, e, s, es_):
                n = t * NX + e
                act.wait_ge(ht_ok, n + 1)
                wait_above_zero(act, dn_ok, n - 1 if es_ >= 2 else t * NX)
                nc.scalar.activation(HS[s][0:HALF, :], bank(2 + s)[0:HALF, 0:2 * P], ACT.Copy).then_inc(hs_ok, 1)

            def experts(t):
                wait_above_zero(act, gu_ok, t * NX)
                act.wait_ge(fx_ok, NT)
                nc.scalar.activation(FT, OA[:, bass.ds(t, 1), :].rearrange("p a n -> p (a n)"), ACT.Copy).then_inc(xs_ok, 1)
                gate(t, 0, 0, 0)
                gate(t, 1, 1, 1)
                copy_hidden(t, 0, 0, 0)
                gate(t, 2, 0, 2)
                copy_hidden(t, 1, 1, 1)
                gate(t, 3, 1, 3)
                copy_hidden(t, 2, 0, 2)
                with act.Fori(0, (NX - 4) // 2) as e2:
                    e = e2 * 2 + 4
                    for s in range(2):
                        gate(t, e + s, s, 4)
                        copy_hidden(t, e + (s - 1), 1 - s, 3)
                copy_hidden(t, NX - 1, 1, NX - 1)

            experts(0)
            with act.Fori(1, NT) as t:
                experts(t)

        @block.vector
        def _(dve):
            v = Chain(dve, vchain, marks)
            dve.wait_ge(x_in, 32)

            def statistics():
                for t in range(NT):
                    v.then(nc.vector.bn_stats(stat[:, :], X[:, t, :]))
                    v.then(nc.vector.bn_aggr(MV[:, t, :], stat[:, :]))

            statistics()
            v.then(nc.vector.tensor_scalar_add(RSTD[:, :], MV[:, :, 1], LN_EPS))
            dve.sem_inc(var_ok, 1)
            dve.wait_ge(sd_ok, 1)
            v.then(nc.vector.reciprocal(RSTD[:, :], SD[:, :]))
            dve.wait_ge(wq_in, 32)
            v.then(nc.vector.tensor_scalar_mul(BQ, BQ, HD ** -0.5))
            dve.wait_ge(consts, 1)

            def normed(dst, t):
                return nc.vector.tensor_scalar(dst, X[:, bass.ds(t, 1), :].rearrange("p a n -> p (a n)"),
                                               MV[:, bass.ds(t, 1), 0:1].rearrange("p a n -> p (a n)"),
                                               RSTD[:, bass.ds(t, 1)], ALU.subtract, ALU.mult)

            def quantise_queries(t):
                normed(XN, t).then_inc(xn_ok, 1)
                dve.wait_ge(q_ok, t + 1)
                v.then(nc.vector.scalar_tensor_tensor(out=QF, in0=bank(7)[:, 0:D], scalar=HD ** -0.5, in1=BQ,
                                                      op0=ALU.mult, op1=ALU.add))
                q3 = QF.rearrange("p (h d) -> p h d", d=HD)
                v.then(nc.vector.tensor_reduce(QAM, q3, axis=AX.X, op=ALU.max, apply_absolute_value=True))
                v.then(nc.vector.tensor_scalar(QAM, QAM, 1.0 / 127.0, FLOOR, ALU.mult, ALU.max))
                v.then(nc.vector.tensor_scalar_mul(NSQ[:, bass.ds(t * H, H)], QAM, -1.0))
                v.then(nc.vector.reciprocal(QRC, QAM))
                v.then(nc.vector.tensor_tensor(q3, q3, QRC.unsqueeze(2).to_broadcast([P, H, HD]), ALU.mult))
                src = QF.rearrange("p (a b d) -> p a b d", b=2, d=HD)
                for part in range(3):
                    dst = QN.rearrange("p (a n) -> p a n", a=PAIRS)
                    for hh in range(2):
                        at = hh * (P + 64) + part * HD
                        v.then(nc.vector.tensor_scalar(dst[:, :, at:at + HD], src[:, :, hh, :], MAGIC, -MAGIC,
                                                       ALU.add, ALU.add))
                dve.sem_inc(qn_ok, 1)

            v.loop(NT, 12, quantise_queries)

            v.then(nc.vector.memset(VM, 0.0))
            dve.wait_ge(wkv_in, 32)

            def quantise_keys(b, s):
                last = isinstance(b, int) and b == NB - 1
                w = WL if last else P
                vst = VST[s].rearrange("w (p j n) -> w p j n", p=PAIRS, j=4)
                if not isinstance(b, int) or b >= 2:
                    dve.wait_ge(v_out[s], (b // 2) * 16)
                for j in range(4):
                    dve.wait_ge(kv_ok, b * 4 + (j + 1))
                    kv = bank(KV_BANKS[j])
                    nc.vector.tensor_tensor(KB[:, j * D:(j + 1) * D], kv[:, 0:D], BKV[:, 0:D], ALU.add)
                    v.then(nc.vector.tensor_tensor(vst[0:w, :, j, :], kv[0:w, D:2 * D].rearrange("w (p n) -> w p n", p=PAIRS),
                                                   BKV[0:w, D:2 * D].rearrange("w (p n) -> w p n", p=PAIRS), ALU.add))
                    dve.sem_inc(kv_used, 1)
                dve.sem_inc(v_ok, 1)
                k3 = KB.rearrange("w (n d) -> w n d", d=HD)
                v.then(nc.vector.tensor_reduce(KAM, k3, axis=AX.X, op=ALU.max, apply_absolute_value=True))
                nc.vector.tensor_reduce(VJ[0:w, :].rearrange("w (p n) -> w p n", p=PAIRS),
                                        vst[0:w].rearrange("w p j n -> w p n j"), axis=AX.X, op=ALU.max,
                                        apply_absolute_value=True)
                v.then(nc.vector.tensor_scalar(KS, KAM, 1.0 / 127.0, FLOOR, ALU.mult, ALU.max))
                v.then(nc.vector.reciprocal(KRC, KS))
                v.then(nc.vector.tensor_tensor(VM[0:w, :], VM[0:w, :], VJ[0:w, :], ALU.max))
                kr = KR.rearrange("w (n d) -> w n d", d=HD)
                v.then(nc.vector.tensor_tensor(kr, k3, KRC.unsqueeze(2).to_broadcast([P, 4 * H, HD]), ALU.mult))
                v.then(nc.vector.tensor_scalar(KR, KR, MAGIC, -MAGIC, ALU.add, ALU.add))
                if not isinstance(b, int) or b >= 2:
                    dve.wait_ge(kn_ok, b - 1)
                    dve.wait_ge(kt_ok, (b - 1) * PAIRS)
                v.then(nc.vector.tensor_tensor(KDQ[s].rearrange("w (n d) -> w n d", d=HD), kr,
                                               KS.unsqueeze(2).to_broadcast([P, 4 * H, HD]), ALU.mult))
                nc.vector.tensor_copy(KN[s].rearrange("w (n d) -> w n d", d=64)[:, :, 0:HD],
                                      KDQ[s].rearrange("w (n d) -> w n d", d=HD)).then_inc(kd_ok, 1)

            per = 11
            for b in range(2):
                quantise_keys(b, b)
            before = v.n
            with dve.Fori(0, (NB - 2 - 2) // 2) as b2:
                b = b2 * 2 + 2
                for s in range(2):
                    v.n = (b - 2) * per + (before + s * per)
                    v.steps = 0
                    quantise_keys(b + s, s)
                    assert v.steps == per, v.steps
            v.n = before + (NB - 4) * per
            quantise_keys(NB - 2, 0)
            quantise_keys(NB - 1, 1)
            dve.wait_ge(qtc_ok, 2 * NT)
            dve.wait_ge(q_out, NT * 16)
            v.then(nc.vector.memset(VS[:, :], 0.0))
            dve.sem_inc(vs_zero, 1)
            dve.sem_inc(vm_ok, 1)
            dve.wait_ge(vmx_ok, 1)
            v.then(nc.vector.tensor_scalar(svb[:, :], svb[:, :], 1.0 / 127.0, FLOOR, ALU.mult, ALU.max))
            v.then(nc.vector.reciprocal(rvb[:, :], svb[:, :]))

            def quantise_values(p, t):
                n = VG * P
                src = VS[:, bass.ds(t * n, n)].rearrange("w (j n) -> w j n", n=32)
                tmp = VT[:, 0:n]
                v.then(nc.vector.tensor_tensor(tmp.rearrange("w (j n) -> w j n", n=32), src,
                                               rvb[:, bass.ds(p * 32, 32)].unsqueeze(1).to_broadcast([P, VG * 4, 32]), ALU.mult))
                v.then(nc.vector.tensor_scalar(VN[:, bass.ds(t * n, n)], tmp, MAGIC, -MAGIC,
                                               ALU.add, ALU.add))
                dve.sem_inc(vq_ok, VG)

            dve.wait_ge(vs_in, 32)
            v.loop(NT, 2, lambda t: quantise_values(0, t))

            def copy_bytes(g, s, fresh=False):
                dve.wait_ge(t_ok, g + 1)
                if not fresh:
                    dve.wait_ge(rb_ok, g - 1)
                nc.vector.tensor_copy(TT[s][:, :], bank(6)[:, 0:CH // 4]).then_inc(tt_ok, 1)

            def maximum(g, c, half, par=0):
                n = BANK if (not isinstance(c, int) or c < NC - 1 or half == 0) else TAIL - BANK
                dve.wait_ge(a_ok, g * 2 + (half + 1))
                nc.vector.tensor_reduce(MX[:, bass.ds(par * NB + c * 2 + half, 1)], bank(4 + half)[:, 0:n], axis=AX.X,
                                        op=ALU.max).then_inc(a_used, 1)

            def item_max(item, hh):
                dve.wait_ge(a_used, item * NB + NB)
                v.begin(nc.vector.tensor_reduce(sm[:, 2:3], MX[:, hh * NB:(hh + 1) * NB], axis=AX.X, op=ALU.max))

            def bias_of(p, t, hh):
                nsq = NSQ[:, bass.ds(t * H + p * 2 + hh, 1)]
                nc.vector.tensor_scalar_mul(BS[:, hh, 1:2], nsq, -1.0)
                v.settle()
                v.then(nc.vector.tensor_scalar(BS[:, hh, 0:1], sm[:, 2:3], nsq, LN255, ALU.mult, ALU.add))
                dve.sem_inc(bias_ok, 1)

            def item_sum(item, hh):
                dve.wait_ge(r_ok, item * NC + NC)
                v.begin(nc.vector.reduce_sum(sm[:, 3:4], ZC[:, hh * NC:(hh + 1) * NC], axis=AX.X))

            def sum_inverse():
                v.settle()
                v.begin(nc.vector.reciprocal(sm[:, 4:5], sm[:, 3:4]))

            def heads_out(item, p, t, hh):
                v.settle()
                dve.wait_ge(pv_ok, item * NC + NC)
                v.then(nc.vector.tensor_scalar_mul(OA[:, bass.ds(t, 1), bass.ds(p * 32 + hh * HD, HD)].rearrange("q a n -> q (a n)"),
                                                   bank(7)[:, 0:HD], sm[:, 4:5]))
                dve.sem_inc(o_used, 1)

            def scale_block(m, p, t, j):
                if j == 0:
                    dve.wait_ge(vs_in, p * 32 + 32)
                dve.wait_ge(vq_ok, m * VG + NT * VG)
                v.begin(nc.vector.tensor_tensor(
                    VT[:, j * P:(j + 1) * P].rearrange("w (j n) -> w j n", n=32),
                    VS[:, bass.ds(t * (VG * P) + j * P, P)].rearrange("w (j n) -> w j n", n=32),
                    rvb[:, bass.ds(p * 32, 32)].unsqueeze(1).to_broadcast([P, 4, 32]), ALU.mult))

            def round_block(t, j):
                v.settle()
                nc.vector.tensor_scalar(VN[:, bass.ds(t * (VG * P) + j * P, P)], VT[:, j * P:(j + 1) * P], MAGIC, -MAGIC,
                                        ALU.add, ALU.add).then_inc(vq_ok, 1)

            def take_values(p):
                v.n, v.steps = p * per_pair + before, 0
                dve.wait_ge(vq_ok, p * (NT * VG) + NT * VG)
                v.then(nc.vector.tensor_copy(VB[:, :], VN[:, :]))
                dve.sem_inc(vb_ok, 1)

            def round_(p, t):
                m = p * NT + t
                pn, tn = next_round(m)
                first = isinstance(t, int) and t == 0
                if not first:
                    v.n = p * per_pair + ((t - 1) * per_round + (before + 1 + per_round - 3))
                v.steps = 0
                for hh in range(2):
                    item = m * 2 + hh
                    g0 = dve.snap(item * NC)
                    fresh = first and hh == 0
                    for c in range(NC):
                        g, s = g0 + c, (c + hh) % 2
                        if not on_scalar((c - LT) % NC) and not (fresh and c < LT):
                            copy_bytes(g - LT, s, fresh and c - LT < 2)
                        if c == LP and not fresh:
                            if hh == 1:
                                heads_out(item - 1, p, t, 0)
                            else:
                                heads_out(item - 1, p, t - 1, 1)
                        par = (1 - hh) if c + LEAD < NC else hh
                        blocks = [j for j in range(VG) if hh == 1 and LP + 1 + j * (NC - LP - 1) // VG == c]
                        maximum(g + (NC + LEAD), c, 0, par)
                        if c == LP - 2 and not fresh:
                            item_sum(item - 1, 1 - hh)
                        if c == NC - LEAD:
                            item_max(item + 1, 1 - hh)
                        for j in blocks:
                            scale_block(m, (p + 1) % PAIRS, t, j)
                        maximum(g + (NC + LEAD), c, 1, par)
                        if c == LP - 2 and not fresh:
                            sum_inverse()
                        if c == NC - LEAD:
                            bias_of(*((p, t, 1) if hh == 0 else (pn, tn, 0)))
                        for j in blocks:
                            round_block(t, j)
                assert v.steps == per_round - (3 if first else 0), v.steps

            def finish(p):
                g = (p + 1) * (2 * NT * NC)
                v.n, v.steps = p * per_pair + (before + per_pair - 3), 0
                for k in range(LT):
                    if not on_scalar(NC - LT + k):
                        copy_bytes(g + (k - LT), k % 2)
                item_sum((p + 1) * (2 * NT) - 1, 1)
                sum_inverse()
                heads_out((p + 1) * (2 * NT) - 1, p, NT - 1, 1)
                assert v.steps == 3

            for half in range(2):
                maximum(0, 0, half)
            with dve.Fori(1, NC - 1) as c:
                for half in range(2):
                    maximum(c, c, half)
            for half in range(2):
                maximum(NC - 1, NC - 1, half)
            item_max(0, 0)
            bias_of(0, 0, 0)
            for c in range(NC - LEAD, NC):
                for half in range(2):
                    maximum(c + LEAD, c, half, 1)
            before = v.n
            per_round = VG + 2 * 2 + 2 * 3
            per_pair = 1 + NT * per_round
            all_rounds(dve, round_, take_values, finish)
            v.n = before + PAIRS * per_pair

            dve.wait_ge(f_in, 48)

            def project_out(t):
                v.then(nc.vector.tensor_tensor(FA, OA[:, bass.ds(t, 1), :].rearrange("p a n -> p (a n)"), svb[:, :], ALU.mult))
                dve.sem_inc(fa_ok, 1)
                xt = X[:, bass.ds(t, 1), :].rearrange("p a n -> p (a n)")
                dve.wait_ge(fm_ok, t + 1)
                v.then(nc.vector.tensor_tensor(YO, bank(1)[:, 0:D], BP, ALU.add))
                v.then(nc.vector.tensor_tensor(xt, xt, YO, ALU.add))

            v.loop(NT, 3, project_out)
            statistics()
            v.then(nc.vector.tensor_scalar_add(RSTD[:, :], MV[:, :, 1], LN_EPS))
            dve.sem_inc(var_ok, 1)
            dve.wait_ge(sd_ok, 2)
            v.then(nc.vector.reciprocal(RSTD[:, :], SD[:, :]))
            v.then(nc.vector.memset(CB, 1.0))
            dve.wait_ge(gw_ok, 1)

            def route(t):
                v.then(normed(FA, t))
                dve.sem_inc(fa_ok, 1)
                dve.wait_ge(fm_ok, t + (NT + 1))
                v.then(nc.vector.tensor_copy(LG, bank(1)[:, 0:E]))
                v.then(nc.vector.tensor_reduce(sm[:, 0:1], LG, axis=AX.X, op=ALU.max, negate=True))
                dve.sem_inc(lm_ok, 1)
                dve.wait_ge(le_ok, t + 1)
                v.then(nc.vector.reciprocal(sm[:, 5:6], sm[:, 1:2]))
                v.then(nc.vector.tensor_scalar_mul(SC, SC, sm[:, 5:6]), apart=True)
                v.then(nc.vector.max(T8, SC), apart=True)
                v.then(nc.vector.max_index(I8, T8, SC))
                v.then(nc.vector.tensor_copy(I8F, I8))
                v.then(nc.vector.tensor_scalar(OH, IO, I8F[:, 0:1], T8[:, 0:1], ALU.is_equal, ALU.mult))
                v.then(nc.vector.tensor_scalar(LG, IO, I8F[:, 1:2], T8[:, 1:2], ALU.is_equal, ALU.mult))
                v.then(nc.vector.tensor_tensor(CB[:, bass.ds(t * NX, E)], OH, LG, ALU.add))

            v.loop(NT, 11, route)

            def hidden(t, e, s, es_):
                n = t * NX + e
                dve.wait_ge(sg_ok, n + 1)
                wait_above_zero(dve, ht_ok, n - 1 if es_ >= 2 else t * NX)
                nc.vector.scalar_tensor_tensor(out=HN[s], in0=bank(s)[:, I:I2], scalar=CB[:, bass.ds(n, 1)], in1=SG[s],
                                               op0=ALU.mult, op1=ALU.mult).then_inc(hn_ok, 1)

            def experts(t):
                hidden(t, 0, 0, 0)
                hidden(t, 1, 1, 1)
                with dve.Fori(0, (NX - 2) // 2) as e2:
                    e = e2 * 2 + 2
                    for s in range(2):
                        hidden(t, e + s, s, 2)
                dve.wait_ge(dn_ok, t * NX + NX)
                wait_above_zero(dve, y_out, t * 16)
                nc.vector.tensor_tensor(YO, X[:, bass.ds(t, 1), :].rearrange("p a n -> p (a n)"), bank(4)[:, 0:D],
                                        ALU.add).then_inc(yo_ok, 1)

            experts(0)
            with dve.Fori(1, NT) as t:
                experts(t)


_INS = ["x", "ctx_2048", "L0_xattn_Wq", "L0_xattn_bq", "L0_xattn_Wkv", "L0_xattn_bkv", "L0_xattn_Wp", "L0_xattn_bp",
        "L0_ffn_gate_w", "L0_ffn_w_gate_up", "L0_ffn_w_down", "L0_ffn_shared_gate_up", "L0_ffn_shared_down"]


def kernel(**inputs):
    import concourse.bacc as bacc
    from concourse.bass_utils import run_bass_kernel_spmd as run

    nc = bacc.Bacc("TRN2", target_bir_lowering=False, num_devices=1)
    arrays, args = {}, []
    for name in _INS:
        a = np.ascontiguousarray(inputs[name])
        arrays[f"in_{name}"] = a
        args.append(nc.dram_tensor(f"in_{name}", a.shape, mybir.dt.from_np(a.dtype), kind="ExternalInput").ap())
    out = nc.dram_tensor("out_0", inputs["x"].shape, F32, kind="ExternalOutput").ap()
    build(nc, *args, out)
    r = run(nc, [arrays], core_ids=[0])
    return r.results[0]["out_0"]
```
